# Optimizing a Trainium2 kernel written in Bass

```python
import numpy as np
import jax
import jax.numpy as jnp

def _softmax(x, axis=-1):
    return jax.nn.softmax(x, axis=axis)

def _gelu(x):
    return jax.nn.gelu(x, approximate=True)

def _silu(x):
    return jax.nn.silu(x)

def _sigmoid(x):
    return jax.nn.sigmoid(x)

def _layernorm(x, axis=-1, eps=1e-05):
    m = jnp.mean(x, axis=axis, keepdims=True)
    v = jnp.var(x, axis=axis, keepdims=True)
    return (x - m) / jnp.sqrt(v + eps)

def _scatter_add(tgt, idx, src, axis=0):
    return tgt.at[idx].add(src)

def _segment_sum(src, seg, n):
    return jax.ops.segment_sum(src, seg, n)
kernel_name = 'mk_gnn_preln_d1_gnn_r32_4359fb'

def setup_inputs(seed: int=0):
    np.random.seed(seed)
    _w = jnp.asarray

    def _rec_inputs():
        import jax
        import jax.numpy as jnp
        _gk = jax.random.key(seed)
        x = -0.0003713 + 1 * jax.random.normal(jax.random.fold_in(_gk, 1), (3125, 128), jnp.float32)
        _s = jax.random.randint(jax.random.fold_in(_gk, 2), (25000,), 0, 3125, jnp.int32)
        _d = jax.random.randint(jax.random.fold_in(_gk, 3), (25000,), 0, 3125, jnp.int32)
        _loop = jnp.arange(3125, dtype=jnp.int32)
        src = jnp.concatenate([_s, _d, _loop])
        dst = jnp.concatenate([_d, _s, _loop])
        _o = jnp.argsort(dst, stable=True)
        src = src[_o]
        dst = dst[_o]
        edge_attr_32 = 0.000312547 + 1.00004 * jax.random.normal(jax.random.fold_in(_gk, 11), (53125, 32), jnp.float32)
        return (x, src, dst, edge_attr_32)
    x, src, dst, edge_attr_32 = _rec_inputs()

    def _L0_gnn_setup():
        import jax, jax.numpy as jnp
        import numpy as np
        N = 3125
        E = 15625
        C_IN = 128
        C_OUT = 128
        C_EDGE = 32
        MESSAGE_STEPS = 2

        def _xavier(key, fan_in, fan_out):
            limit = float(np.sqrt(6.0 / (fan_in + fan_out)))
            return jax.random.uniform(key, (fan_in, fan_out), jnp.float32, -limit, limit)
        key = jax.random.key(seed)
        k = jax.random.split(key, 6)
        x = jax.random.normal(k[0], (N, C_IN), jnp.float32)
        edge_index = jax.random.randint(k[1], (2, E), 0, N, jnp.int64)
        edge_attr = jax.random.normal(k[2], (E, C_EDGE), jnp.float32)
        We1 = _xavier(k[3], 2 * C_IN + C_EDGE, C_OUT)
        be1 = jnp.zeros((C_OUT,), jnp.float32)
        We2 = _xavier(k[4], C_OUT, C_OUT)
        be2 = jnp.zeros((C_OUT,), jnp.float32)
        bias = jnp.zeros((C_OUT,), jnp.float32)
        return {'x': x, 'edge_index': edge_index, 'edge_attr': edge_attr, 'We1': We1, 'be1': be1, 'We2': We2, 'be2': be2, 'bias': bias}
    _L0_gnn_all = _L0_gnn_setup()
    _L0_gnn_in = {k: v for k, v in _L0_gnn_all.items() if k in ('We1', 'be1', 'We2', 'be2', 'bias')}
    del _L0_gnn_all
    return {'x': x, 'src': src, 'dst': dst, 'edge_attr_32': edge_attr_32, 'L0_gnn_We1': _L0_gnn_in['We1'], 'L0_gnn_be1': _L0_gnn_in['be1'], 'L0_gnn_We2': _L0_gnn_in['We2'], 'L0_gnn_be2': _L0_gnn_in['be2'], 'L0_gnn_bias': _L0_gnn_in['bias']}

def reference(x, src, dst, edge_attr_32, L0_gnn_We1, L0_gnn_be1, L0_gnn_We2, L0_gnn_be2, L0_gnn_bias):
    import jax
    import jax.numpy as jnp

    def _L0_gnn_ref(x, edge_index, edge_attr, We1, be1, We2, be2, bias):
        import jax, jax.numpy as jnp
        import numpy as np
        N = 3125
        E = 15625
        C_IN = 128
        C_OUT = 128
        C_EDGE = 32
        MESSAGE_STEPS = 2

        def _xavier(key, fan_in, fan_out):
            limit = float(np.sqrt(6.0 / (fan_in + fan_out)))
            return jax.random.uniform(key, (fan_in, fan_out), jnp.float32, -limit, limit)
        ei = edge_index[0]
        ej = edge_index[1]
        h = x
        for _ in range(MESSAGE_STEPS):
            h_i = h[ei]
            h_j = h[ej]
            edge_input = jnp.concatenate([h_i, h_j, edge_attr], axis=-1)
            m_ij = jax.nn.relu(edge_input @ We1 + be1) @ We2 + be2
            m = jax.ops.segment_sum(m_ij, ej, num_segments=N)
            h = h + m
        return h + bias
    edge_index = jnp.stack([src, dst])
    h = jnp.maximum(_layernorm(x, axis=-1), 0.0)
    x = x + _L0_gnn_ref(h, edge_index, edge_attr_32, L0_gnn_We1, L0_gnn_be1, L0_gnn_We2, L0_gnn_be2, L0_gnn_bias)
    return x

_drawn_inputs = setup_inputs


def setup_inputs(seed=0):
    import zlib

    import numpy as np

    out = dict(_drawn_inputs(seed))
    spreads = {'L0_gnn_be1': (0.0, 0.1), 'L0_gnn_be2': (0.0, 0.1), 'L0_gnn_bias': (0.0, 0.1)}
    factors = {}
    for name, (base, spread) in spreads.items():
        noise = np.random.default_rng([zlib.crc32(name.encode()), seed]).standard_normal(out[name].shape)
        drawn = base * np.exp(spread * noise) if base else spread * noise
        out[name] = jnp.asarray(drawn.astype(out[name].dtype))
    for name, factor in factors.items():
        out[name] = (out[name] * factor).astype(out[name].dtype)
    return out
```

```python
import concourse.bass as bass
from concourse import mybir
from contextlib import ExitStack

N = 3125
E = 53125
C = 128
CE = 32
STEPS = 2
P = 128

NODE_TILES = -(-N // P)
NP = NODE_TILES * P
TILES = 4
EDGE_GROUP = TILES * P
GROUPS = -(-E // EDGE_GROUP)
EP = GROUPS * EDGE_GROUP
WINDOW = 64
U = 4
ITERS = GROUPS // U
MB = 2
BATCH = 4
BATCHES = [(b, min(BATCH, NODE_TILES - b)) for b in range(0, NODE_TILES, BATCH)]
CHUNK = NP // 8
EPS = 1e-5
assert GROUPS % U == 0 and NP % 8 == 0 and CHUNK <= 512 and N + WINDOW <= NP


def gnn_kernel(nc, x, src_groups, dst_groups, dst_row, group_base, edge_t, we1, be1, we2, be2, bias, p_tab, q_tab, out):
    fp32, bf16, i32 = mybir.dt.float32, mybir.dt.bfloat16, mybir.dt.int32
    ALU = mybir.AluOpType
    ACT = mybir.ActivationFunctionType
    AX = mybir.AxisListType

    x_v = x.rearrange("(t p) c -> p t c", p=P)
    out_v = out.rearrange("(t p) c -> p t c", p=P)
    p_v = [t.rearrange("(t p) c -> p t c", p=P) for t in p_tab]
    q_v = [t.rearrange("(t p) c -> p t c", p=P) for t in q_tab]

    ctx = ExitStack()
    with ctx:
        def sb(name, shape, dt=fp32):
            return ctx.enter_context(nc.sbuf_tensor(name, shape, dt))

        def sem(name):
            return ctx.enter_context(nc.semaphore(name))

        ident = sb("ident", [P, P])
        ones = sb("ones", [P, 1])
        iota_nodes = sb("iota_nodes", [P, NP])
        iota_part = sb("iota_part", [P, 1])
        w1sd = sb("w1sd", [C, 2, C])
        w2 = sb("w2", [C, C])
        be1_all = sb("be1_all", [P, C])
        tail_rows = sb("tail_rows", [2, C])
        x_sb = sb("x_sb", [P, NODE_TILES, C])
        norm = sb("norm", [P, NODE_TILES, C])
        stage = sb("stage", [P, NODE_TILES, C])
        hT = [sb(f"hT{s}", [C, NP]) for s in range(STEPS)]
        msgT = [sb(f"msgT{s}", [C, NP]) for s in range(STEPS)]
        deg_one = sb("deg_one", [2, NP])
        stats = sb("stats", [P, NODE_TILES, 6])
        mv = sb("mv", [P, NODE_TILES, 2])
        rstd = sb("rstd", [P, NODE_TILES, 1])
        dst_pt = sb("dst_pt", [P, GROUPS, TILES], i32)
        rel = sb("rel", [P, GROUPS, TILES])
        base_all = sb("base_all", [P, GROUPS], i32)
        window_node = sb("window_node", [WINDOW, GROUPS])
        extremes = sb("extremes", [P, 3])
        outside = sb("outside", [1, 1], i32)
        lhs = sb("lhs", [WINDOW + CE, U, EDGE_GROUP])
        rhs = sb("rhs", [WINDOW + CE, U, C])
        dst_rows = sb("dst_rows", [WINDOW, U, EDGE_GROUP], i32)
        src_idx = sb("src_idx", [P, U, TILES], i32)
        gath = sb("gath", [P, U, TILES, C])
        act_in = sb("act_in", [P, U, TILES, C])
        onehot = sb("onehot", [P, U, TILES, WINDOW])
        dst_f = sb("dst_f", [P, TILES])
        onehot_all = sb("onehot_all", [P, NP])
        bank = [ctx.enter_context(nc.psum_tensor(f"bank{b}", [P, 512], fp32)) for b in range(8)]

        x_in = [sem(f"x_in{b}") for b in range(len(BATCHES))]
        weights_in = sem("weights_in")
        tables_in = sem("tables_in")
        ident_zero = sem("ident_zero")
        ident_ready = sem("ident_ready")
        consts_ready = sem("consts_ready")
        deg_ready = sem("deg_ready")
        msg_zero = sem("msg_zero")
        stats_done = sem("stats_done")
        std_done = sem("std_done")
        rstd_done = sem("rstd_done")
        norm_done = sem("norm_done")
        transposed = sem("transposed")
        hT0_done = sem("hT0_done")
        p_prod = sem("p_prod")
        q_prod = sem("q_prod")
        p_staged = sem("p_staged")
        q_staged = sem("q_staged")
        p_stored = [sem(f"p_stored{s}") for s in range(STEPS)]
        q_stored = [sem(f"q_stored{s}") for s in range(STEPS)]
        dve_chain = sem("dve_chain")
        extremes_ready = sem("extremes_ready")
        outside_sum = sem("outside_sum")
        outside_ready = sem("outside_ready")
        dstrow_in = [sem(f"dstrow_in{u}") for u in range(U)]
        window_in = [sem(f"window_in{u}") for u in range(U)]
        idx_in = [sem(f"idx_in{u}") for u in range(U)]
        groups_started = sem("groups_started")
        gathered = [sem(f"gathered{u}") for u in range(U)]
        onehots_built = sem("onehots_built")
        pre_done = sem("pre_done")
        sum_done = sem("sum_done")
        relu_done = sem("relu_done")
        msgs_summed = sem("msgs_summed")
        msgs_added = sem("msgs_added")
        degs_added = sem("degs_added")
        gen_in = sem("gen_in")
        gen_gathered = sem("gen_gathered")
        gen_pre = sem("gen_pre")
        gen_onehot = sem("gen_onehot")
        gen_summed = sem("gen_summed")
        gen_added = sem("gen_added")
        gen_group_done = sem("gen_group_done")
        step_done = sem("step_done")
        update_prod = sem("update_prod")
        updated = sem("updated")
        final_prod = sem("final_prod")
        final_done = sem("final_done")
        stored = sem("stored")
        marker = sb("marker", [1, 1])

        W_DMAS, T_DMAS = 6 + U, 3

        block = ctx.enter_context(nc.Block())

        def outside_flag(eng):
            eng.wait_ge(outside_ready, 1)
            return eng.value_load(outside[0:1, 0:1], min_val=0, max_val=P)

        @block.sync
        def _(sp):
            for b, (t0, n) in enumerate(BATCHES):
                sp.dma_start(x_sb[:, t0:t0 + n, :], x_v[:, t0:t0 + n, :]).then_inc(x_in[b], 16)
            sp.dma_start(w1sd[:, :, :], we1[0:2 * C, :].rearrange("(k p) c -> p k c", k=2)).then_inc(weights_in, 16)
            sp.dma_start(w2[:, :], we2).then_inc(weights_in, 16)
            sp.dma_start(be1_all[:, :], be1.to_broadcast([P, C])).then_inc(weights_in, 16)
            sp.dma_start(tail_rows[0:1, :], be2).then_inc(weights_in, 16)
            sp.dma_start(tail_rows[1:2, :], bias).then_inc(weights_in, 16)
            for u in range(U):
                sp.dma_start(rhs[WINDOW:WINDOW + CE, u, :], we1[2 * C:2 * C + CE, :]).then_inc(weights_in, 16)
            sp.dma_start(marker[0:1, 0:1], bias[0:1, 0:1]).then_inc(weights_in, 16)
            sp.dma_start(dst_pt[:, :, :], dst_groups.rearrange("g p j -> p g j")).then_inc(tables_in, 16)
            sp.dma_start(base_all[:, :], group_base.to_broadcast([P, GROUPS])).then_inc(tables_in, 16)
            sp.dma_start(dst_rows[:, 0, 0:1], dst_row[0:1, 0:1].to_broadcast([WINDOW, 1])).then_inc(tables_in, 16)

            def store_tables(s):
                for b, (t0, n) in enumerate(BATCHES):
                    seq = s * len(BATCHES) + b + 1
                    sp.wait_ge(p_staged, seq)
                    sp.dma_start(p_v[s][:, t0:t0 + n, :], stage[:, t0:t0 + n, :]).then_inc(p_stored[s], 16)
                    sp.wait_ge(q_staged, seq)
                    sp.dma_start(q_v[s][:, t0:t0 + n, :], norm[:, t0:t0 + n, :]).then_inc(q_stored[s], 16)

            def windowed_group(s, i, u, first):
                k = i * U + u
                done = s * GROUPS + k
                if not first:
                    sp.wait_ge(onehots_built, done - U + 1)
                sp.dma_start(dst_rows[:, u, :],
                             dst_row[0:1, bass.ds(k * EDGE_GROUP, EDGE_GROUP)].to_broadcast([WINDOW, EDGE_GROUP])
                             ).then_inc(dstrow_in[u], 16)
                if not first:
                    sp.wait_ge(gathered[u], TILES * 16 * (s * ITERS + i))
                sp.dma_start(src_idx[:, u, :], src_groups[bass.ds(k, 1), :, :].rearrange("g p j -> p (g j)")
                             ).then_inc(idx_in[u], 16)
                base = sp.value_load(base_all[0:1, bass.ds(k, 1)], min_val=0, max_val=N)
                if not first:
                    sp.wait_ge(pre_done, done - U + 1)
                sp.dma_start(lhs[WINDOW:WINDOW + CE, u, :], edge_t[:, bass.ds(k * EDGE_GROUP, EDGE_GROUP)]
                             ).then_inc(window_in[u], 16)
                sp.dma_start(rhs[0:WINDOW, u, :], q_tab[s][bass.ds(base, WINDOW), :]).then_inc(window_in[u], 16)

            def general_group(s, g):
                seq = s * GROUPS + g
                sp.wait_ge(gen_group_done, seq + 1)
                sp.dma_start(src_idx[:, 0, :], src_groups[bass.ds(g, 1), :, :].rearrange("g p j -> p (g j)")
                             ).then_inc(gen_in, 16)
                sp.dma_start(src_idx[:, 1, :], dst_groups[bass.ds(g, 1), :, :].rearrange("g p j -> p (g j)")
                             ).then_inc(gen_in, 16)
                sp.dma_start(lhs[WINDOW:WINDOW + CE, 0, :], edge_t[:, bass.ds(g * EDGE_GROUP, EDGE_GROUP)]
                             ).then_inc(gen_in, 16)

            flag = outside_flag(sp)
            for s in range(STEPS):
                store_tables(s)
                sp.wait_ge(q_stored[s], 16 * len(BATCHES))
                with sp.If(flag == 0):
                    for u in range(U):
                        windowed_group(s, 0, u, s == 0)
                    with sp.Fori(1, ITERS) as i:
                        for u in range(U):
                            windowed_group(s, i, u, False)
                with sp.Else():
                    with sp.Fori(0, GROUPS) as g:
                        general_group(s, g)
            for b, (t0, n) in enumerate(BATCHES):
                sp.wait_ge(final_done, b + 1)
                sp.dma_start(out_v[:, t0:t0 + n, :], stage[:, t0:t0 + n, :]).then_inc(stored, 16)
            sp.wait_ge(stored, 16 * len(BATCHES))

        @block.gpsimd
        def _(pool):
            nc.gpsimd.memset(ident[:, :], 0.0).then_inc(ident_zero, 1)
            pool.wait_ge(ident_zero, 1)
            nc.gpsimd.affine_select(out=ident[:, :], in_=ident[:, :], compare_op=ALU.not_equal, fill=1.0, base=0,
                                    pattern=[[-1, P]], channel_multiplier=1).then_inc(ident_ready, 1)
            nc.gpsimd.iota(iota_part[:, :], pattern=[[0, 1]], base=0, channel_multiplier=1,
                           allow_small_or_imprecise_dtypes=True)
            nc.gpsimd.iota(iota_nodes[:, :], pattern=[[1, NP]], base=0, channel_multiplier=0,
                           allow_small_or_imprecise_dtypes=True)
            nc.gpsimd.memset(ones[:, :], 1.0).then_inc(consts_ready, 1)
            nc.gpsimd.memset(deg_one[:, :], 1.0).then_inc(deg_ready, 1)
            pool.wait_ge(deg_ready, 1)
            nc.gpsimd.memset(deg_one[0:1, :], 0.0).then_inc(msg_zero, 1)
            for s in range(STEPS):
                nc.gpsimd.memset(msgT[s][:, :], 0.0).then_inc(msg_zero, 1)

            def windowed_group(s, i, u, first):
                if not first:
                    pool.wait_ge(sum_done, s * GROUPS + i * U + u - U + 1)
                pool.wait_ge(idx_in[u], 16 * (s * ITERS + i + 1))
                pool.sem_inc(groups_started, 1)
                for j in range(TILES):
                    nc.gpsimd.indirect_dma_start(gath[:, u, j, :], None, p_tab[s],
                                                 bass.IndirectOffsetOnAxis(ap=src_idx[:, u, j:j + 1], axis=0)
                                                 ).then_inc(gathered[u], 16)

            def general_group(s, g):
                seq = s * GROUPS + g
                pool.wait_ge(gen_in, 48 * (seq + 1))
                pool.sem_inc(groups_started, 1)
                for k, tab in enumerate((p_tab[s], q_tab[s])):
                    for j in range(TILES):
                        nc.gpsimd.indirect_dma_start(gath[:, k, j, :], None, tab,
                                                     bass.IndirectOffsetOnAxis(ap=src_idx[:, k, j:j + 1], axis=0)
                                                     ).then_inc(gen_gathered, 16)

            flag = outside_flag(pool)
            for s in range(STEPS):
                pool.wait_ge(p_stored[s], 16 * len(BATCHES))
                with pool.If(flag == 0):
                    for u in range(U):
                        windowed_group(s, 0, u, s == 0)
                    with pool.Fori(1, ITERS) as i:
                        for u in range(U):
                            windowed_group(s, i, u, False)
                with pool.Else():
                    pool.wait_ge(q_stored[s], 16 * len(BATCHES))
                    with pool.Fori(0, GROUPS) as g:
                        general_group(s, g)

        @block.scalar
        def _(act):
            act.wait_ge(stats_done, 1)
            nc.scalar.activation(rstd[:, :, :], mv[:, :, 1:2], ACT.Sqrt).then_inc(std_done, 1)

            def stage_p(s, b, t0, n):
                act.wait_ge(p_prod, s * len(BATCHES) + b + 1)
                if s >= 1 and b == 0:
                    act.wait_ge(p_stored[s - 1], 16 * len(BATCHES))
                nc.scalar.activation(stage[:, t0:t0 + n, :],
                                     bank[b % 2][:, 0:n * C].rearrange("p (t c) -> p t c", c=C), ACT.Copy
                                     ).then_inc(p_staged, 1)

            for b, (t0, n) in enumerate(BATCHES):
                act.wait_ge(transposed, b + 1)
                nc.scalar.activation(hT[0][:, t0 * P:(t0 + n) * P], bank[4 + b % 2][:, 0:n * P], ACT.Relu
                                     ).then_inc(hT0_done, 1)
                if b >= 1:
                    stage_p(0, b - 1, *BATCHES[b - 1])
            stage_p(0, len(BATCHES) - 1, *BATCHES[-1])

            def relu_group(s, i, u, first):
                done = s * GROUPS + i * U + u
                act.wait_ge(sum_done, done + 1)
                nc.scalar.activation(act_in[:, u, :, :], act_in[:, u, :, :], ACT.Relu).then_inc(relu_done, 1)

            flag = outside_flag(act)
            for s in range(STEPS):
                if s >= 1:
                    for b, (t0, n) in enumerate(BATCHES):
                        stage_p(s, b, t0, n)
                with act.If(flag == 0):
                    with act.Fori(0, ITERS) as i:
                        for u in range(U):
                            relu_group(s, i, u, False)
                with act.Else():
                    act.wait_ge(gen_group_done, 1)

        @block.tensor
        def _(pe):
            pe.wait_ge(ident_ready, 1)
            pe.wait_ge(weights_in, 16 * W_DMAS)

            def project(s, b, t0, n):
                seq = s * len(BATCHES) + b
                for which, prod, staged in ((0, p_prod, p_staged), (1, q_prod, q_staged)):
                    if b >= 2:
                        pe.wait_ge(staged, seq - 1)
                    for j in range(n):
                        t = t0 + j
                        last = nc.tensor.matmul(bank[2 * which + b % 2][:, j * C:(j + 1) * C],
                                                hT[s][:, t * P:(t + 1) * P], w1sd[:, which, :], start=True, stop=True)
                    last.then_inc(prod, 1)

            def transpose(b, t0, n):
                pe.wait_ge(norm_done, b + 1)
                if b >= 2:
                    pe.wait_ge(hT0_done, b - 1)
                for j in range(n):
                    last = nc.tensor.transpose(bank[4 + b % 2][:, j * P:(j + 1) * P], norm[:, t0 + j, :], ident[:, :])
                last.then_inc(transposed, 1)

            pe.wait_ge(extremes_ready, 1)
            nc.tensor.matmul(bank[7][0:1, 0:1], extremes[:, 2:3], ones[:, :], start=True, stop=True
                             ).then_inc(outside_sum, 1)
            for b, (t0, n) in enumerate(BATCHES):
                transpose(b, t0, n)
                if b >= 1:
                    pe.wait_ge(hT0_done, b)
                    project(0, b - 1, *BATCHES[b - 1])
            pe.wait_ge(hT0_done, len(BATCHES))
            project(0, len(BATCHES) - 1, *BATCHES[-1])

            def pre_activation(s, i, u, first):
                done = s * GROUPS + i * U + u
                pe.wait_ge(window_in[u], 32 * (s * ITERS + i + 1))
                pe.wait_ge(onehots_built, done + 1)
                if not first:
                    pe.wait_ge(sum_done, done - U + 1)
                for j in range(TILES):
                    last = nc.tensor.matmul(bank[u][:, j * C:(j + 1) * C], lhs[:, u, j * P:(j + 1) * P], rhs[:, u, :],
                                            start=True, stop=True)
                last.then_inc(pre_done, 1)

            def sum_messages(s, seq, u, first):
                pe.wait_ge(relu_done, seq + 1)
                if not first:
                    pe.wait_ge(msgs_added, seq - MB + 1)
                m = bank[4 + u % MB]
                for j in range(TILES):
                    last = nc.tensor.matmul(m[:, 0:WINDOW], act_in[:, u, j, :], onehot[:, u, j, :],
                                            start=(j == 0), stop=(j == TILES - 1))
                if s == 0:
                    for j in range(TILES):
                        half = onehot[:, u, j, :].bitcast(bf16).rearrange("p (n two) -> p n two", two=2)[:, :, 1]
                        last = nc.tensor.matmul(m[0:1, WINDOW:2 * WINDOW],
                                                ones[:, :].bitcast(bf16)[:, 1:2], half,
                                                start=(j == 0), stop=(j == TILES - 1))
                last.then_inc(msgs_summed, 1)

            def windowed_iteration(s, i, first):
                for u in range(U):
                    pre_activation(s, i, u, first and s == 0)
                    if u >= 2 or not first:
                        seq = s * GROUPS + i * U + u - 2
                        sum_messages(s, seq, (u - 2) % U, first and s == 0 and u - 2 < MB)

            def general_group(s, g):
                seq = s * GROUPS + g
                pe.wait_ge(gen_in, 48 * (seq + 1))
                for j in range(TILES):
                    last = nc.tensor.matmul(bank[0][:, j * C:(j + 1) * C],
                                            lhs[WINDOW:WINDOW + CE, 0, j * P:(j + 1) * P],
                                            rhs[WINDOW:WINDOW + CE, 0, :], start=True, stop=True)
                last.then_inc(gen_pre, 1)
                per_group = TILES * (2 if s == 0 else 1)
                sums_before = g * per_group + (0 if s == 0 else 2 * TILES * GROUPS)
                for j in range(TILES):
                    pe.wait_ge(gen_onehot, seq * TILES + j + 1)
                    for k in range(8):
                        last = nc.tensor.matmul(bank[k][:, 0:CHUNK], act_in[:, 0, j, :],
                                                onehot_all[:, k * CHUNK:(k + 1) * CHUNK], start=True, stop=True)
                    last.then_inc(gen_summed, 1)
                    if s == 0:
                        pe.wait_ge(gen_added, sums_before + 2 * j + 1)
                        for k in range(8):
                            last = nc.tensor.matmul(bank[k][0:1, 0:CHUNK], ones[:, :],
                                                    onehot_all[:, k * CHUNK:(k + 1) * CHUNK], start=True, stop=True)
                        last.then_inc(gen_summed, 1)

            flag = outside_flag(pe)
            for s in range(STEPS):
                with pe.If(flag == 0):
                    pe.wait_ge(p_staged, (s + 1) * len(BATCHES))
                    pe.wait_ge(q_staged, (s + 1) * len(BATCHES))
                    windowed_iteration(s, 0, True)
                    with pe.Fori(1, ITERS) as i:
                        windowed_iteration(s, i, False)
                    for seq in (GROUPS - 2, GROUPS - 1):
                        sum_messages(s, s * GROUPS + seq, seq % U, False)
                with pe.Else():
                    pe.wait_ge(p_staged, (s + 1) * len(BATCHES))
                    pe.wait_ge(q_staged, (s + 1) * len(BATCHES))
                    with pe.Fori(0, GROUPS) as g:
                        general_group(s, g)
                pe.wait_ge(step_done, s + 1)
                if s == 0:
                    for k in range(8):
                        nc.tensor.matmul(bank[k][:, 0:CHUNK], w2[:, :], msgT[0][:, k * CHUNK:(k + 1) * CHUNK],
                                         start=True, stop=False)
                        nc.tensor.matmul(bank[k][:, 0:CHUNK], tail_rows[0:1, :],
                                         deg_one[0:1, k * CHUNK:(k + 1) * CHUNK],
                                         start=False, stop=True).then_inc(update_prod, 1)
                    for b, (t0, n) in enumerate(BATCHES):
                        pe.wait_ge(updated, 8)
                        project(1, b, t0, n)
            for b, (t0, n) in enumerate(BATCHES):
                if b >= 4:
                    pe.wait_ge(final_done, b - 3)
                for j in range(n):
                    o = bank[b % 4][:, j * C:(j + 1) * C]
                    nodes = slice((t0 + j) * P, (t0 + j + 1) * P)
                    nc.tensor.matmul(o, hT[1][:, nodes], ident[:, :], start=True, stop=False)
                    nc.tensor.matmul(o, msgT[1][:, nodes], w2[:, :], start=False, stop=False)
                    last = nc.tensor.matmul(o, deg_one[:, nodes], tail_rows[:, :], start=False, stop=True)
                last.then_inc(final_prod, 1)

        @block.vector
        def _(dve):
            chain = [0]

            def link(ins):
                chain[0] += 1
                ins.then_inc(dve_chain, 1)
                dve.wait_ge(dve_chain, chain[0])

            dve.wait_ge(tables_in, 16 * T_DMAS)
            dve.wait_ge(consts_ready, 1)
            link(nc.vector.tensor_tensor(rel[:, :, :], dst_pt[:, :, :],
                                         base_all[:, :].unsqueeze(2).to_broadcast([P, GROUPS, TILES]), ALU.subtract))
            nc.vector.tensor_scalar(window_node[:, :], base_all[0:WINDOW, :], iota_part[0:WINDOW, :], None, ALU.add)
            nc.vector.tensor_reduce(extremes[:, 0:1], rel[:, :, :].rearrange("p g j -> p (g j)"), AX.X, ALU.max)
            link(nc.vector.tensor_reduce(extremes[:, 1:2], rel[:, :, :].rearrange("p g j -> p (g j)"), AX.X, ALU.min))
            link(nc.vector.tensor_scalar(extremes[:, 1:2], extremes[:, 1:2], 0.0, None, ALU.is_lt))
            nc.vector.scalar_tensor_tensor(extremes[:, 2:3], extremes[:, 0:1], float(WINDOW - 1), extremes[:, 1:2],
                                           ALU.is_gt, ALU.add).then_inc(extremes_ready, 1)
            for b, (t0, n) in enumerate(BATCHES):
                dve.wait_ge(x_in[b], 16)
                for t in range(t0, t0 + n):
                    last = nc.vector.bn_stats(stats[:, t, :], x_sb[:, t, :])
            link(last)
            dve.wait_ge(outside_sum, 1)
            nc.vector.tensor_copy(outside[:, :], bank[7][0:1, 0:1]).then_inc(outside_ready, 1)
            for t in range(NODE_TILES):
                last = nc.vector.bn_aggr(mv[:, t, :], stats[:, t, :])
            link(last)
            nc.vector.tensor_scalar(mv[:, :, 1:2], mv[:, :, 1:2], EPS, None, ALU.add).then_inc(stats_done, 1)
            dve.wait_ge(std_done, 1)
            link(nc.vector.reciprocal(rstd[:, :, :], rstd[:, :, :]))
            for b, (t0, n) in enumerate(BATCHES):
                for t in range(t0, t0 + n):
                    last = nc.vector.tensor_scalar(norm[:, t, :], x_sb[:, t, :], mv[:, t, 0:1], rstd[:, t, :],
                                                   ALU.subtract, ALU.mult)
                last.then_inc(norm_done, 1)

            def stage_q(s):
                for b, (t0, n) in enumerate(BATCHES):
                    dve.wait_ge(q_prod, s * len(BATCHES) + b + 1)
                    if s >= 1 and b == 0:
                        dve.wait_ge(q_stored[s - 1], 16 * len(BATCHES))
                    if s == 0:
                        dve.wait_ge(transposed, b + 1)
                    nc.vector.tensor_tensor(norm[:, t0:t0 + n, :],
                                            bank[2 + b % 2][:, 0:n * C].rearrange("p (t c) -> p t c", c=C),
                                            be1_all[:, :].unsqueeze(1).to_broadcast([P, n, C]), ALU.add
                                            ).then_inc(q_staged, 1)

            def build_onehots(s, i, u, first):
                k = i * U + u
                done = s * GROUPS + k
                dve.wait_ge(dstrow_in[u], 16 * (s * ITERS + i + 1))
                if not first:
                    dve.wait_ge(pre_done, done - U + 1)
                nc.vector.tensor_scalar(lhs[0:WINDOW, u, :], dst_rows[:, u, :],
                                        window_node[:, bass.ds(k, 1)], None, ALU.is_equal)
                if not first:
                    dve.wait_ge(msgs_summed, done - U + 1)
                nc.vector.tensor_tensor(onehot[:, u, :, :],
                                        rel[:, bass.ds(k, 1), :].rearrange("p g j -> p (g j)").unsqueeze(2)
                                        .to_broadcast([P, TILES, WINDOW]),
                                        iota_nodes[:, 0:WINDOW].unsqueeze(1).to_broadcast([P, TILES, WINDOW]),
                                        ALU.is_equal).then_inc(onehots_built, 1)

            def add_gathered(s, seq, it, u, first):
                dve.wait_ge(pre_done, seq + 1)
                dve.wait_ge(gathered[u], TILES * 16 * (it + 1))
                if not first:
                    dve.wait_ge(msgs_summed, seq - U + 2)
                nc.vector.tensor_tensor(act_in[:, u, :, :].rearrange("p j c -> p (j c)"), bank[u][:, :],
                                        gath[:, u, :, :].rearrange("p j c -> p (j c)"), ALU.add
                                        ).then_inc(sum_done, 1)

            def add_messages(s, k, seq, u, first):
                base = dve.value_load(base_all[0:1, bass.ds(k, 1)], min_val=0, max_val=N)
                dve.wait_ge(msgs_summed, seq + 1)
                if not first:
                    dve.wait_ge(msgs_added, seq)
                if s == 0:
                    nc.vector.tensor_tensor(deg_one[0:1, bass.ds(base, WINDOW)], deg_one[0:1, bass.ds(base, WINDOW)],
                                            bank[4 + u % MB][0:1, WINDOW:2 * WINDOW], ALU.add)
                nc.vector.tensor_tensor(msgT[s][:, bass.ds(base, WINDOW)], msgT[s][:, bass.ds(base, WINDOW)],
                                        bank[4 + u % MB][:, 0:WINDOW], ALU.add).then_inc(msgs_added, 1)

            def windowed_iteration(s, i, first):
                for u in range(U):
                    build_onehots(s, i, u, first and s == 0)
                    if u >= 1 or not first:
                        seq = s * GROUPS + i * U + u - 1
                        it = s * ITERS + i - (u < 1)
                        add_gathered(s, seq, it, (u - 1) % U, first and s == 0)
                    if u >= 3 or not first:
                        k = i * U + u - 3
                        add_messages(s, k, s * GROUPS + k, (u - 3) % U, first and s == 0 and u == 3)

            def general_group(s, g):
                seq = s * GROUPS + g
                dve.wait_ge(gen_pre, seq + 1)
                dve.wait_ge(gen_gathered, 2 * TILES * 16 * (seq + 1))
                nc.vector.tensor_copy(dst_f[:, :], src_idx[:, 1, :])
                a = act_in[:, 0, :, :].rearrange("p j c -> p (j c)")
                glink(nc.vector.tensor_tensor(a, bank[0][:, :], gath[:, 0, :, :].rearrange("p j c -> p (j c)"),
                                              ALU.add), s, g)
                glink(nc.vector.tensor_tensor(a, a, gath[:, 1, :, :].rearrange("p j c -> p (j c)"), ALU.add), s, g)
                glink(nc.vector.tensor_scalar(a, a, 0.0, None, ALU.max), s, g)
                per_group = TILES * (2 if s == 0 else 1)
                sums_before = g * per_group + (0 if s == 0 else 2 * TILES * GROUPS)
                for j in range(TILES):
                    nc.vector.tensor_scalar(onehot_all[:, :], iota_nodes[:, :], dst_f[:, j:j + 1], None,
                                            ALU.is_equal).then_inc(gen_onehot, 1)
                    n = j * (2 if s == 0 else 1)
                    dve.wait_ge(gen_summed, sums_before + n + 1)
                    for k in range(8):
                        m = msgT[s][:, k * CHUNK:(k + 1) * CHUNK]
                        last = nc.vector.tensor_tensor(m, m, bank[k][:, 0:CHUNK], ALU.add)
                    last.then_inc(gen_added, 1)
                    dve.wait_ge(gen_added, sums_before + n + 1)
                    if s == 0:
                        dve.wait_ge(gen_summed, sums_before + n + 2)
                        for k in range(8):
                            d = deg_one[0:1, k * CHUNK:(k + 1) * CHUNK]
                            last = nc.vector.tensor_tensor(d, d, bank[k][0:1, 0:CHUNK], ALU.add)
                        last.then_inc(gen_added, 1)
                        dve.wait_ge(gen_added, sums_before + n + 2)
                nc.vector.memset(marker[:, :], 0.0).then_inc(gen_group_done, 1)

            links = [0]

            def glink(ins, s, g):
                ins.then_inc(degs_added, 1)
                links[0] = links[0] % 3 + 1
                dve.wait_ge(degs_added, 3 * (s * GROUPS + g) + links[0])

            flag = outside_flag(dve)
            dve.wait_ge(msg_zero, 1 + STEPS)
            for s in range(STEPS):
                stage_q(s)
                with dve.If(flag == 0):
                    windowed_iteration(s, 0, True)
                    with dve.Fori(1, ITERS) as i:
                        windowed_iteration(s, i, False)
                    last_group = s * GROUPS + GROUPS - 1
                    add_gathered(s, last_group, s * ITERS + ITERS - 1, U - 1, False)
                    for k in range(GROUPS - 3, GROUPS):
                        add_messages(s, k, s * GROUPS + k, k % U, False)
                    dve.wait_ge(msgs_added, (s + 1) * GROUPS)
                with dve.Else():
                    if s == 0:
                        nc.vector.memset(marker[:, :], 0.0).then_inc(gen_group_done, 1)
                    with dve.Fori(0, GROUPS) as g:
                        general_group(s, g)
                    dve.wait_ge(gen_group_done, (s + 1) * GROUPS + 1)
                nc.vector.memset(marker[:, :], 0.0).then_inc(step_done, 1)
                if s == 0:
                    for k in range(8):
                        nodes = slice(k * CHUNK, (k + 1) * CHUNK)
                        dve.wait_ge(update_prod, k + 1)
                        nc.vector.tensor_tensor(hT[1][:, nodes], hT[0][:, nodes], bank[k][:, 0:CHUNK], ALU.add
                                                ).then_inc(updated, 1)
            for b, (t0, n) in enumerate(BATCHES):
                dve.wait_ge(final_prod, b + 1)
                if b == 0:
                    dve.wait_ge(p_stored[STEPS - 1], 16 * len(BATCHES))
                nc.vector.tensor_tensor(stage[:, t0:t0 + n, :],
                                        bank[b % 4][:, 0:n * C].rearrange("p (t c) -> p t c", c=C),
                                        x_sb[:, t0:t0 + n, :], ALU.add).then_inc(final_done, 1)


def kernel(x, src, dst, edge_attr_32, L0_gnn_We1, L0_gnn_be1, L0_gnn_We2, L0_gnn_be2, L0_gnn_bias):
    import numpy as np
    import concourse.bacc as bacc
    from concourse.bass_utils import run_bass_kernel_spmd as run

    def padded(a, rows, fill=0):
        a = np.asarray(a)
        return np.concatenate([a, np.full((rows - a.shape[0], *a.shape[1:]), fill, a.dtype)])

    src = padded(src, EP)
    dst = padded(dst, EP, N)
    row = lambda a: np.asarray(a).reshape(1, -1)
    arrays = {
        "x": padded(x, NP),
        "src_groups": np.ascontiguousarray(src.reshape(GROUPS, TILES, P).transpose(0, 2, 1)),
        "dst_groups": np.ascontiguousarray(dst.reshape(GROUPS, TILES, P).transpose(0, 2, 1)),
        "dst_row": row(dst),
        "group_base": row(dst[::EDGE_GROUP].copy()),
        "edge_t": np.ascontiguousarray(padded(edge_attr_32, EP).T),
        "we1": np.asarray(L0_gnn_We1), "be1": row(L0_gnn_be1), "we2": np.asarray(L0_gnn_We2),
        "be2": row(L0_gnn_be2), "bias": row(L0_gnn_bias),
    }
    nc = bacc.Bacc("TRN2", target_bir_lowering=False, num_devices=1)
    args = {k: nc.dram_tensor(k, a.shape, mybir.dt.from_np(a.dtype), kind="ExternalInput").ap()
            for k, a in arrays.items()}
    tables = {k: [nc.dram_tensor(f"{k}{s}", (NP, C), mybir.dt.float32, kind="Internal").ap() for s in range(STEPS)]
              for k in ("p_tab", "q_tab")}
    out = nc.dram_tensor("out", (NP, C), mybir.dt.float32, kind="ExternalOutput").ap()
    gnn_kernel(nc, **args, **tables, out=out)
    return run(nc, [arrays], core_ids=[0]).results[0]["out"][:N]
```

```python
import concourse.bass as bass
from concourse import mybir
from contextlib import ExitStack

N = 3125
E = 53125
C = 128
CE = 32
STEPS = 2
P = 128

NODE_TILES = -(-N // P)
NP = NODE_TILES * P
TILES = 4
EDGE_GROUP = TILES * P
GROUPS = -(-E // EDGE_GROUP)
EP = GROUPS * EDGE_GROUP
WINDOW = 64
U = 4
ITERS = GROUPS // U
LAG = 3
MB = 2
BATCH = 4
BATCHES = [(b, min(BATCH, NODE_TILES - b)) for b in range(0, NODE_TILES, BATCH)]
K_PRE = WINDOW + CE + 1
CHUNK = NP // 8
EPS = 1e-5
TAIL_TILES = range(ITERS - LAG, NODE_TILES)
assert GROUPS % U == 0 and NP % 8 == 0 and CHUNK <= 512 and N + WINDOW <= NP


def gnn_kernel(nc, x, src_groups, dst_groups, dst_row, group_base, edge_t, we1, be1, we2, be2, bias, p_tab, q_tab, out):
    fp32, bf16, i32 = mybir.dt.float32, mybir.dt.bfloat16, mybir.dt.int32
    ALU = mybir.AluOpType
    ACT = mybir.ActivationFunctionType
    AX = mybir.AxisListType

    x_v = x.rearrange("(t p) c -> p t c", p=P)
    p_v = [t.rearrange("(t p) c -> p t c", p=P) for t in p_tab]
    q_v = [t.rearrange("(t p) c -> p t c", p=P) for t in q_tab]

    ctx = ExitStack()
    with ctx:
        def sb(name, shape, dt=fp32):
            return ctx.enter_context(nc.sbuf_tensor(name, shape, dt))

        def sem(name):
            return ctx.enter_context(nc.semaphore(name))

        ident = sb("ident", [P, P])
        ones = sb("ones", [P, 1])
        iota_nodes = sb("iota_nodes", [P, NP])
        iota_part = sb("iota_part", [P, 1])
        w1sd = sb("w1sd", [C, 2, C])
        w2 = sb("w2", [C, C])
        tail_rows = sb("tail_rows", [2, C])
        x_sb = sb("x_sb", [P, NODE_TILES, C])
        norm = sb("norm", [P, NODE_TILES, C])
        stage = sb("stage", [P, NODE_TILES, C])
        hT = sb("hT", [C, NP])
        h_tile = sb("h_tile", [C, P])
        tile_out = sb("tile_out", [P, 2, C])
        msgT = [sb(f"msgT{s}", [C, NP]) for s in range(STEPS)]
        deg_one = sb("deg_one", [2, NP])
        stats = sb("stats", [P, NODE_TILES, 6])
        mv = sb("mv", [P, NODE_TILES, 2])
        rstd = sb("rstd", [P, NODE_TILES, 1])
        dst_pt = sb("dst_pt", [P, GROUPS, TILES], i32)
        rel = sb("rel", [P, GROUPS, TILES])
        base_all = sb("base_all", [P, GROUPS], i32)
        window_node = sb("window_node", [WINDOW, GROUPS])
        first_node = sb("first_node", [P, GROUPS, TILES])
        early = sb("early", [P, GROUPS, TILES])
        extremes = sb("extremes", [P, 4])
        outside = sb("outside", [1, 1], i32)
        lhs = sb("lhs", [K_PRE, U, EDGE_GROUP])
        rhs = sb("rhs", [K_PRE, U, C])
        dst_rows = sb("dst_rows", [WINDOW, U, EDGE_GROUP], i32)
        src_idx = sb("src_idx", [P, U, TILES], i32)
        gath = sb("gath", [P, U, TILES, C])
        act_in = sb("act_in", [P, U, TILES, C])
        onehot = sb("onehot", [P, U, TILES, WINDOW])
        dst_f = sb("dst_f", [P, TILES])
        onehot_all = sb("onehot_all", [P, NP])
        bank = [ctx.enter_context(nc.psum_tensor(f"bank{b}", [P, 512], fp32)) for b in range(8)]

        x_in = [sem(f"x_in{b}") for b in range(len(BATCHES))]
        weights_in = sem("weights_in")
        tables_in = sem("tables_in")
        ident_zero = sem("ident_zero")
        ident_ready = sem("ident_ready")
        consts_ready = sem("consts_ready")
        deg_ready = sem("deg_ready")
        bias_ready = sem("bias_ready")
        msg_zero = sem("msg_zero")
        stats_done = sem("stats_done")
        std_done = sem("std_done")
        norm_done = sem("norm_done")
        transposed = sem("transposed")
        hT0_done = sem("hT0_done")
        p_prod = sem("p_prod")
        q_prod = sem("q_prod")
        p_staged = sem("p_staged")
        q_staged = sem("q_staged")
        p_stored = [sem(f"p_stored{s}") for s in range(STEPS)]
        q_stored = [sem(f"q_stored{s}") for s in range(STEPS)]
        dve_chain = sem("dve_chain")
        extremes_ready = sem("extremes_ready")
        outside_sum = sem("outside_sum")
        outside_ready = sem("outside_ready")
        dstrow_in = [sem(f"dstrow_in{u}") for u in range(U)]
        window_in = [sem(f"window_in{u}") for u in range(U)]
        idx_in = [sem(f"idx_in{u}") for u in range(U)]
        groups_started = sem("groups_started")
        gathered = [sem(f"gathered{u}") for u in range(U)]
        onehots_built = sem("onehots_built")
        pre_done = sem("pre_done")
        sum_done = sem("sum_done")
        relu_done = sem("relu_done")
        msgs_summed = sem("msgs_summed")
        msgs_added = sem("msgs_added")
        gen_link = sem("gen_link")
        gen_in = sem("gen_in")
        gen_gathered = sem("gen_gathered")
        gen_pre = sem("gen_pre")
        gen_onehot = sem("gen_onehot")
        gen_summed = sem("gen_summed")
        gen_added = sem("gen_added")
        gen_group_done = sem("gen_group_done")
        step_done = sem("step_done")
        update_prod = sem("update_prod")
        updated = sem("updated")
        h_kept = sem("h_kept")
        tile_prod = sem("tile_prod")
        tile_staged = sem("tile_staged")
        stored = sem("stored")
        marker = sb("marker", [1, 1])

        TABLE_DMAS = [len(BATCHES)] + [NODE_TILES] * (STEPS - 1)
        W_DMAS, T_DMAS = 4 + 2 * U, 2

        block = ctx.enter_context(nc.Block())

        def outside_flag(eng):
            eng.wait_ge(outside_ready, 1)
            return eng.value_load(outside[0:1, 0:1], min_val=0, max_val=2 * P)

        @block.sync
        def _(sp):
            def load_x(b, t0, n):
                sp.dma_start(x_sb[:, t0:t0 + n, :], x_v[:, t0:t0 + n, :]).then_inc(x_in[b], 16)

            load_x(0, *BATCHES[0])
            sp.dma_start(dst_pt[:, :, :], dst_groups).then_inc(tables_in, 16)
            sp.dma_start(base_all[:, :], group_base.to_broadcast([P, GROUPS])).then_inc(tables_in, 16)
            for b in range(1, len(BATCHES)):
                load_x(b, *BATCHES[b])
            sp.dma_start(w1sd[:, :, :], we1[0:2 * C, :].rearrange("(k p) c -> p k c", k=2)).then_inc(weights_in, 16)
            for u in range(U):
                sp.dma_start(rhs[WINDOW:WINDOW + CE, u, :], we1[2 * C:2 * C + CE, :]).then_inc(weights_in, 16)
                sp.dma_start(rhs[WINDOW + CE:K_PRE, u, :], be1).then_inc(weights_in, 16)
            sp.dma_start(w2[:, :], we2).then_inc(weights_in, 16)
            sp.dma_start(tail_rows[0:1, :], be2).then_inc(weights_in, 16)
            sp.dma_start(tail_rows[1:2, :], bias).then_inc(weights_in, 16)

            def store_tables():
                for b, (t0, n) in enumerate(BATCHES):
                    sp.wait_ge(p_staged, b + 1)
                    sp.dma_start(p_v[0][:, t0:t0 + n, :], stage[:, t0:t0 + n, :]).then_inc(p_stored[0], 16)
                for b, (t0, n) in enumerate(BATCHES):
                    sp.wait_ge(q_staged, b + 1)
                    sp.dma_start(q_v[0][:, t0:t0 + n, :], norm[:, t0:t0 + n, :]).then_inc(q_stored[0], 16)

            def windowed_group(s, i, u, first):
                k = i * U + u
                done = s * GROUPS + k
                if not first:
                    sp.wait_ge(onehots_built, done - U + 1)
                sp.dma_start(dst_rows[:, u, :],
                             dst_row[0:1, bass.ds(k * EDGE_GROUP, EDGE_GROUP)].to_broadcast([WINDOW, EDGE_GROUP])
                             ).then_inc(dstrow_in[u], 16)
                if not first:
                    sp.wait_ge(gathered[u], TILES * 16 * (s * ITERS + i))
                sp.dma_start(src_idx[:, u, :], src_groups[:, bass.ds(k, 1), :].rearrange("p g j -> p (g j)")
                             ).then_inc(idx_in[u], 16)
                base = sp.value_load(base_all[0:1, bass.ds(k, 1)], min_val=0, max_val=N)
                if not first:
                    sp.wait_ge(pre_done, done - U + 1)
                sp.dma_start(lhs[WINDOW:WINDOW + CE, u, :], edge_t[:, bass.ds(k * EDGE_GROUP, EDGE_GROUP)]
                             ).then_inc(window_in[u], 16)
                if isinstance(i, int) and u == 0:
                    sp.wait_ge(q_stored[s], 16 * TABLE_DMAS[s])
                sp.dma_start(rhs[0:WINDOW, u, :], q_tab[s][bass.ds(base, WINDOW), :]).then_inc(window_in[u], 16)

            def general_group(s, g):
                seq = s * GROUPS + g
                sp.wait_ge(gen_group_done, seq + 1)
                sp.dma_start(src_idx[:, 0, :], src_groups[:, bass.ds(g, 1), :].rearrange("p g j -> p (g j)")
                             ).then_inc(gen_in, 16)
                sp.dma_start(src_idx[:, 1, :], dst_groups[:, bass.ds(g, 1), :].rearrange("p g j -> p (g j)")
                             ).then_inc(gen_in, 16)
                sp.dma_start(lhs[WINDOW:WINDOW + CE, 0, :], edge_t[:, bass.ds(g * EDGE_GROUP, EDGE_GROUP)]
                             ).then_inc(gen_in, 16)

            store_tables()
            flag = outside_flag(sp)
            for s in range(STEPS):
                with sp.If(flag == 0):
                    for u in range(U):
                        windowed_group(s, 0, u, s == 0)
                    with sp.Fori(1, ITERS) as i:
                        for u in range(U):
                            windowed_group(s, i, u, False)
                with sp.Else():
                    with sp.Fori(0, GROUPS) as g:
                        general_group(s, g)

        @block.gpsimd
        def _(pool):
            nc.gpsimd.memset(ident[:, :], 0.0).then_inc(ident_zero, 1)
            pool.wait_ge(ident_zero, 1)
            nc.gpsimd.affine_select(out=ident[:, :], in_=ident[:, :], compare_op=ALU.not_equal, fill=1.0, base=0,
                                    pattern=[[-1, P]], channel_multiplier=1).then_inc(ident_ready, 1)
            nc.gpsimd.iota(iota_part[:, :], pattern=[[0, 1]], base=0, channel_multiplier=1,
                           allow_small_or_imprecise_dtypes=True)
            nc.gpsimd.iota(iota_nodes[:, :], pattern=[[1, NP]], base=0, channel_multiplier=0,
                           allow_small_or_imprecise_dtypes=True)
            nc.gpsimd.iota(first_node[:, :, :].rearrange("p (i u) j -> p i (u j)", u=U), pattern=[[P, ITERS], [0, U * TILES]],
                           base=-(LAG - 1) * P, channel_multiplier=0, allow_small_or_imprecise_dtypes=True)
            nc.gpsimd.memset(ones[:, :], 1.0).then_inc(consts_ready, 1)
            pool.wait_ge(consts_ready, 1)
            nc.gpsimd.memset(lhs[WINDOW + CE:K_PRE, :, :], 1.0).then_inc(bias_ready, 1)
            pool.wait_ge(bias_ready, 1)
            nc.gpsimd.memset(deg_one[:, :], 1.0).then_inc(deg_ready, 1)
            pool.wait_ge(deg_ready, 1)
            nc.gpsimd.memset(deg_one[0:1, :], 0.0).then_inc(msg_zero, 1)
            for s in range(STEPS):
                nc.gpsimd.memset(msgT[s][:, :], 0.0).then_inc(msg_zero, 1)

            def windowed_group(s, i, u, first):
                if not first:
                    pool.wait_ge(sum_done, s * GROUPS + i * U + u - U + 1)
                pool.wait_ge(idx_in[u], 16 * (s * ITERS + i + 1))
                pool.sem_inc(groups_started, 1)
                for j in range(TILES):
                    nc.gpsimd.indirect_dma_start(gath[:, u, j, :], None, p_tab[s],
                                                 bass.IndirectOffsetOnAxis(ap=src_idx[:, u, j:j + 1], axis=0)
                                                 ).then_inc(gathered[u], 16)

            def general_group(s, g):
                seq = s * GROUPS + g
                pool.wait_ge(gen_in, 48 * (seq + 1))
                pool.sem_inc(groups_started, 1)
                for k, tab in enumerate((p_tab[s], q_tab[s])):
                    for j in range(TILES):
                        nc.gpsimd.indirect_dma_start(gath[:, k, j, :], None, tab,
                                                     bass.IndirectOffsetOnAxis(ap=src_idx[:, k, j:j + 1], axis=0)
                                                     ).then_inc(gen_gathered, 16)

            flag = outside_flag(pool)
            for s in range(STEPS):
                pool.wait_ge(p_stored[s], 16 * TABLE_DMAS[s])
                with pool.If(flag == 0):
                    for u in range(U):
                        windowed_group(s, 0, u, s == 0)
                    with pool.Fori(1, ITERS) as i:
                        for u in range(U):
                            windowed_group(s, i, u, False)
                with pool.Else():
                    pool.wait_ge(q_stored[s], 16 * TABLE_DMAS[s])
                    with pool.Fori(0, GROUPS) as g:
                        general_group(s, g)

        @block.scalar
        def _(act):
            def stage_table(b, t0, n, banks, prod, staged, to):
                act.wait_ge(prod, b + 1)
                nc.scalar.activation(to[:, t0:t0 + n, :],
                                     bank[banks + b % 2][:, 0:n * C].rearrange("p (t c) -> p t c", c=C), ACT.Copy
                                     ).then_inc(staged, 1)

            def root(b, t0, n):
                act.wait_ge(stats_done, b + 1)
                nc.scalar.activation(rstd[:, t0:t0 + n, :], mv[:, t0:t0 + n, 1:2], ACT.Sqrt).then_inc(std_done, 1)

            root(0, *BATCHES[0])
            root(1, *BATCHES[1])
            for b, (t0, n) in enumerate(BATCHES):
                if b + 2 < len(BATCHES):
                    root(b + 2, *BATCHES[b + 2])
                act.wait_ge(transposed, b + 1)
                nc.scalar.activation(hT[:, t0 * P:(t0 + n) * P], bank[4 + b % 2][:, 0:n * P], ACT.Relu
                                     ).then_inc(hT0_done, 1)
                if b >= 1:
                    stage_table(b - 1, *BATCHES[b - 1], 0, p_prod, p_staged, stage)
            stage_table(len(BATCHES) - 1, *BATCHES[-1], 0, p_prod, p_staged, stage)
            for b, (t0, n) in enumerate(BATCHES):
                stage_table(b, t0, n, 2, q_prod, q_staged, norm)

            def relu_group(s, i, u):
                act.wait_ge(sum_done, s * GROUPS + i * U + u + 1)
                nc.scalar.activation(act_in[:, u, :, :], act_in[:, u, :, :], ACT.Relu).then_inc(relu_done, 1)

            def send_tile(s, t, first):
                seq = s * NODE_TILES + t
                act.wait_ge(tile_prod, seq + 1)
                if s < STEPS - 1:
                    if not first:
                        act.wait_ge(p_stored[s + 1], 16 * t)
                        act.wait_ge(q_stored[s + 1], 16 * t)
                    nc.scalar.activation(tile_out[:, :, :], bank[7][:, 0:2 * C].rearrange("p (k c) -> p k c", k=2),
                                         ACT.Copy).then_inc(tile_staged, 1)
                    act.wait_ge(tile_staged, seq + 1)
                    act.dma_start(p_tab[s + 1][bass.ds(t * P, P), :], tile_out[:, 0, :]).then_inc(p_stored[s + 1], 16)
                    act.dma_start(q_tab[s + 1][bass.ds(t * P, P), :], tile_out[:, 1, :]).then_inc(q_stored[s + 1], 16)
                else:
                    if not first:
                        act.wait_ge(stored, 16 * t)
                    nc.scalar.activation(tile_out[:, 0, :], bank[7][:, 0:C], ACT.Copy).then_inc(tile_staged, 1)
                    act.wait_ge(tile_staged, seq + 1)
                    act.dma_start(out[bass.ds(t * P, P), :], tile_out[:, 0, :]).then_inc(stored, 16)

            def windowed_iteration(s, i, tile, first_tile=False):
                for u in range(U):
                    if u == U - 1 and tile:
                        send_tile(s, i - LAG, first_tile)
                    relu_group(s, i, u)

            flag = outside_flag(act)
            for s in range(STEPS):
                with act.If(flag == 0):
                    with act.Fori(0, LAG) as i:
                        windowed_iteration(s, i, False)
                    windowed_iteration(s, LAG, True, True)
                    with act.Fori(LAG + 1, ITERS) as i:
                        windowed_iteration(s, i, True)
                    for t in TAIL_TILES:
                        send_tile(s, t, False)
                with act.Else():
                    send_tile(s, 0, True)
                    with act.Fori(1, NODE_TILES) as t:
                        send_tile(s, t, False)
                if s < STEPS - 1:
                    act.wait_ge(p_stored[s + 1], 16 * NODE_TILES)
                    act.wait_ge(q_stored[s + 1], 16 * NODE_TILES)
            act.wait_ge(stored, 16 * NODE_TILES)

        @block.tensor
        def _(pe):
            pe.wait_ge(ident_ready, 1)
            pe.wait_ge(consts_ready, 1)

            def project(which, b, t0, n, prod, staged):
                if b >= 2:
                    pe.wait_ge(staged, b - 1)
                for j in range(n):
                    t = t0 + j
                    last = nc.tensor.matmul(bank[2 * which + b % 2][:, j * C:(j + 1) * C],
                                            hT[:, t * P:(t + 1) * P], w1sd[:, which, :], start=True, stop=True)
                last.then_inc(prod, 1)

            def transpose(b, t0, n):
                pe.wait_ge(norm_done, b + 1)
                if b >= 2:
                    pe.wait_ge(hT0_done, b - 1)
                for j in range(n):
                    last = nc.tensor.transpose(bank[4 + b % 2][:, j * P:(j + 1) * P], norm[:, t0 + j, :], ident[:, :])
                last.then_inc(transposed, 1)

            for b, (t0, n) in enumerate(BATCHES):
                transpose(b, t0, n)
                if b == 1:
                    pe.wait_ge(extremes_ready, 1)
                    nc.tensor.matmul(bank[7][0:1, 0:1], extremes[:, 3:4], ones[:, :], start=True, stop=True
                                     ).then_inc(outside_sum, 1)
                    pe.wait_ge(weights_in, 16 * W_DMAS)
                if b >= 1:
                    pe.wait_ge(hT0_done, b)
                    project(0, b - 1, *BATCHES[b - 1], p_prod, p_staged)
            pe.wait_ge(hT0_done, len(BATCHES))
            project(0, len(BATCHES) - 1, *BATCHES[-1], p_prod, p_staged)
            for b, (t0, n) in enumerate(BATCHES):
                project(1, b, t0, n, q_prod, q_staged)

            def pre_activation(s, i, u, first):
                done = s * GROUPS + i * U + u
                pe.wait_ge(window_in[u], 32 * (s * ITERS + i + 1))
                pe.wait_ge(onehots_built, done + 1)
                if not first:
                    pe.wait_ge(sum_done, done - U + 1)
                for j in range(TILES):
                    last = nc.tensor.matmul(bank[u][:, j * C:(j + 1) * C], lhs[:, u, j * P:(j + 1) * P], rhs[:, u, :],
                                            start=True, stop=True)
                last.then_inc(pre_done, 1)

            def sum_messages(s, seq, u, first):
                pe.wait_ge(relu_done, seq + 1)
                if not first:
                    pe.wait_ge(msgs_added, seq - MB + 1)
                m = bank[4 + u % MB]
                for j in range(TILES):
                    last = nc.tensor.matmul(m[:, 0:WINDOW], act_in[:, u, j, :], onehot[:, u, j, :],
                                            start=(j == 0), stop=(j == TILES - 1))
                if s == 0:
                    for j in range(TILES):
                        half = onehot[:, u, j, :].bitcast(bf16).rearrange("p (n two) -> p n two", two=2)[:, :, 1]
                        last = nc.tensor.matmul(m[0:1, WINDOW:2 * WINDOW],
                                                ones[:, :].bitcast(bf16)[:, 1:2], half,
                                                start=(j == 0), stop=(j == TILES - 1))
                last.then_inc(msgs_summed, 1)

            def update_tile(s, t, first):
                nodes = bass.ds(t * P, P)
                if not first:
                    pe.wait_ge(updated, s * NODE_TILES + t)
                rows = 1 if s < STEPS - 1 else 2
                nc.tensor.matmul(bank[6][:, 0:P], w2[:, :], msgT[s][:, nodes], start=True, stop=False)
                nc.tensor.matmul(bank[6][:, 0:P], tail_rows[0:rows, :], deg_one[0:rows, nodes],
                                 start=False, stop=True).then_inc(update_prod, 1)

            def finish_tile(s, t, first):
                seq = s * NODE_TILES + t
                pe.wait_ge(updated, seq + 1)
                if not first:
                    pe.wait_ge(tile_staged, seq)
                if s < STEPS - 1:
                    last = nc.tensor.matmul(bank[7][:, 0:2 * C], h_tile[:, :],
                                            w1sd[:, :, :].rearrange("p k c -> p (k c)"), start=True, stop=True)
                else:
                    nc.tensor.matmul(bank[7][:, 0:C], h_tile[:, :], ident[:, :], start=True, stop=False)
                    last = nc.tensor.matmul(bank[7][:, 0:C], ident[:, :],
                                            x_sb[:, bass.ds(t, 1), :].rearrange("p t c -> p (t c)"),
                                            start=False, stop=True)
                last.then_inc(tile_prod, 1)

            def windowed_iteration(s, i, first, tile, first_tile=False):
                for u in range(U):
                    if u == U - 1 and tile:
                        pe.wait_ge(msgs_added, s * GROUPS + i * U)
                        update_tile(s, i - LAG, first_tile and s == 0)
                    pre_activation(s, i, u, first and s == 0)
                    if u >= 2 or not first:
                        seq = s * GROUPS + i * U + u - 2
                        sum_messages(s, seq, (u - 2) % U, first and s == 0 and u - 2 < MB)
                if tile:
                    finish_tile(s, i - LAG, first_tile and s == 0)

            def general_group(s, g):
                seq = s * GROUPS + g
                pe.wait_ge(gen_in, 48 * (seq + 1))
                for j in range(TILES):
                    last = nc.tensor.matmul(bank[0][:, j * C:(j + 1) * C],
                                            lhs[WINDOW:K_PRE, 0, j * P:(j + 1) * P],
                                            rhs[WINDOW:K_PRE, 0, :], start=True, stop=True)
                last.then_inc(gen_pre, 1)
                per_group = TILES * (2 if s == 0 else 1)
                sums_before = g * per_group + (0 if s == 0 else 2 * TILES * GROUPS)
                for j in range(TILES):
                    pe.wait_ge(gen_onehot, seq * TILES + j + 1)
                    for k in range(8):
                        last = nc.tensor.matmul(bank[k][:, 0:CHUNK], act_in[:, 0, j, :],
                                                onehot_all[:, k * CHUNK:(k + 1) * CHUNK], start=True, stop=True)
                    last.then_inc(gen_summed, 1)
                    if s == 0:
                        pe.wait_ge(gen_added, sums_before + 2 * j + 1)
                        for k in range(8):
                            last = nc.tensor.matmul(bank[k][0:1, 0:CHUNK], ones[:, :],
                                                    onehot_all[:, k * CHUNK:(k + 1) * CHUNK], start=True, stop=True)
                        last.then_inc(gen_summed, 1)

            flag = outside_flag(pe)
            pe.wait_ge(bias_ready, 1)
            pe.wait_ge(p_staged, len(BATCHES))
            pe.wait_ge(q_staged, len(BATCHES))
            for s in range(STEPS):
                with pe.If(flag == 0):
                    windowed_iteration(s, 0, True, False)
                    with pe.Fori(1, LAG) as i:
                        windowed_iteration(s, i, False, False)
                    windowed_iteration(s, LAG, False, True, True)
                    with pe.Fori(LAG + 1, ITERS) as i:
                        windowed_iteration(s, i, False, True)
                    for k in (GROUPS - 2, GROUPS - 1):
                        sum_messages(s, s * GROUPS + k, k % U, False)
                    pe.wait_ge(msgs_added, (s + 1) * GROUPS)
                    for t in TAIL_TILES:
                        update_tile(s, t, False)
                        finish_tile(s, t, False)
                with pe.Else():
                    with pe.Fori(0, GROUPS) as g:
                        general_group(s, g)
                    pe.wait_ge(step_done, s + 1)
                    update_tile(s, 0, s == 0)
                    finish_tile(s, 0, s == 0)
                    with pe.Fori(1, NODE_TILES) as t:
                        update_tile(s, t, False)
                        finish_tile(s, t, False)

        @block.vector
        def _(dve):
            chain = [0]

            def link(ins):
                chain[0] += 1
                ins.then_inc(dve_chain, 1)
                dve.wait_ge(dve_chain, chain[0])

            def tile_stats(b, t0, n):
                dve.wait_ge(x_in[b], 16)
                for t in range(t0, t0 + n):
                    last = nc.vector.bn_stats(stats[:, t, :], x_sb[:, t, :])
                link(last)
                for t in range(t0, t0 + n):
                    last = nc.vector.bn_aggr(mv[:, t, :], stats[:, t, :])
                link(last)
                nc.vector.tensor_scalar(mv[:, t0:t0 + n, 1:2], mv[:, t0:t0 + n, 1:2], EPS, None, ALU.add
                                        ).then_inc(stats_done, 1)

            def normalize(b, t0, n):
                dve.wait_ge(std_done, b + 1)
                link(nc.vector.reciprocal(rstd[:, t0:t0 + n, :], rstd[:, t0:t0 + n, :]))
                for t in range(t0, t0 + n):
                    last = nc.vector.tensor_scalar(norm[:, t, :], x_sb[:, t, :], mv[:, t, 0:1], rstd[:, t, :],
                                                   ALU.subtract, ALU.mult)
                last.then_inc(norm_done, 1)

            def check_edges():
                flat = lambda a: a[:, :, :].rearrange("p g j -> p (g j)")
                dve.wait_ge(tables_in, 16 * T_DMAS)
                dve.wait_ge(consts_ready, 1)
                nc.vector.tensor_tensor(rel[:, :, :], dst_pt[:, :, :],
                                        base_all[:, :].unsqueeze(2).to_broadcast([P, GROUPS, TILES]), ALU.subtract)
                nc.vector.tensor_scalar(window_node[:, :], base_all[0:WINDOW, :], iota_part[0:WINDOW, :], None,
                                        ALU.add)
                link(nc.vector.tensor_tensor(flat(early), flat(dst_pt), flat(first_node), ALU.is_lt))
                nc.vector.tensor_reduce(extremes[:, 0:1], flat(rel), AX.X, ALU.max)
                nc.vector.tensor_reduce(extremes[:, 1:2], flat(rel), AX.X, ALU.min)
                link(nc.vector.tensor_reduce(extremes[:, 2:3], flat(early), AX.X, ALU.max))
                link(nc.vector.scalar_tensor_tensor(extremes[:, 2:3], extremes[:, 1:2], 0.0, extremes[:, 2:3],
                                                    ALU.is_lt, ALU.add))
                nc.vector.scalar_tensor_tensor(extremes[:, 3:4], extremes[:, 0:1], float(WINDOW - 1),
                                               extremes[:, 2:3], ALU.is_gt, ALU.add).then_inc(extremes_ready, 1)

            tile_stats(0, *BATCHES[0])
            for b, (t0, n) in enumerate(BATCHES):
                if b + 1 < len(BATCHES):
                    tile_stats(b + 1, *BATCHES[b + 1])
                normalize(b, t0, n)
                if b == 1:
                    check_edges()
            dve.wait_ge(outside_sum, 1)
            nc.vector.tensor_copy(outside[:, :], bank[7][0:1, 0:1]).then_inc(outside_ready, 1)

            def build_onehots(s, i, u, first):
                k = i * U + u
                done = s * GROUPS + k
                dve.wait_ge(dstrow_in[u], 16 * (s * ITERS + i + 1))
                if not first:
                    dve.wait_ge(pre_done, done - U + 1)
                nc.vector.tensor_scalar(lhs[0:WINDOW, u, :], dst_rows[:, u, :],
                                        window_node[:, bass.ds(k, 1)], None, ALU.is_equal)
                if not first:
                    dve.wait_ge(msgs_summed, done - U + 1)
                nc.vector.tensor_tensor(onehot[:, u, :, :],
                                        rel[:, bass.ds(k, 1), :].rearrange("p g j -> p (g j)").unsqueeze(2)
                                        .to_broadcast([P, TILES, WINDOW]),
                                        iota_nodes[:, 0:WINDOW].unsqueeze(1).to_broadcast([P, TILES, WINDOW]),
                                        ALU.is_equal).then_inc(onehots_built, 1)

            def add_gathered(s, seq, it, u, first):
                dve.wait_ge(pre_done, seq + 1)
                dve.wait_ge(gathered[u], TILES * 16 * (it + 1))
                if not first:
                    dve.wait_ge(msgs_summed, seq - U + 2)
                nc.vector.tensor_tensor(act_in[:, u, :, :].rearrange("p j c -> p (j c)"), bank[u][:, :],
                                        gath[:, u, :, :].rearrange("p j c -> p (j c)"), ALU.add
                                        ).then_inc(sum_done, 1)

            def add_messages(s, k, seq, u, first):
                base = dve.value_load(base_all[0:1, bass.ds(k, 1)], min_val=0, max_val=N)
                dve.wait_ge(msgs_summed, seq + 1)
                if not first:
                    dve.wait_ge(msgs_added, seq)
                if s == 0:
                    nc.vector.tensor_tensor(deg_one[0:1, bass.ds(base, WINDOW)], deg_one[0:1, bass.ds(base, WINDOW)],
                                            bank[4 + u % MB][0:1, WINDOW:2 * WINDOW], ALU.add)
                nc.vector.tensor_tensor(msgT[s][:, bass.ds(base, WINDOW)], msgT[s][:, bass.ds(base, WINDOW)],
                                        bank[4 + u % MB][:, 0:WINDOW], ALU.add).then_inc(msgs_added, 1)

            def update_h(s, t, first):
                seq = s * NODE_TILES + t
                nodes = bass.ds(t * P, P)
                dve.wait_ge(update_prod, seq + 1)
                if not first:
                    dve.wait_ge(tile_prod, seq)
                    dve.wait_ge(h_kept, min(seq, NODE_TILES) if isinstance(seq, int) else seq if s == 0 else NODE_TILES)
                if s < STEPS - 1:
                    nc.vector.tensor_tensor(h_tile[:, :], hT[:, nodes], bank[6][:, 0:P], ALU.add
                                            ).then_inc(updated, 1)
                    dve.wait_ge(updated, seq + 1)
                    nc.vector.tensor_scalar(hT[:, nodes], h_tile[:, :], 1.0, None, ALU.mult
                                            ).then_inc(h_kept, 1)
                else:
                    nc.vector.tensor_tensor(h_tile[:, :], hT[:, nodes], bank[6][:, 0:P], ALU.add
                                            ).then_inc(updated, 1)

            def windowed_iteration(s, i, first, tile, first_tile=False):
                for u in range(U):
                    build_onehots(s, i, u, first and s == 0)
                    if u >= 1 or not first:
                        seq = s * GROUPS + i * U + u - 1
                        it = s * ITERS + i - (u < 1)
                        add_gathered(s, seq, it, (u - 1) % U, first and s == 0)
                    if u >= 3 or not first:
                        k = i * U + u - 3
                        add_messages(s, k, s * GROUPS + k, (u - 3) % U, first and s == 0 and u == 3)
                if tile:
                    update_h(s, i - LAG, first_tile and s == 0)

            def general_group(s, g):
                seq = s * GROUPS + g
                dve.wait_ge(gen_pre, seq + 1)
                dve.wait_ge(gen_gathered, 2 * TILES * 16 * (seq + 1))
                nc.vector.tensor_copy(dst_f[:, :], src_idx[:, 1, :])
                a = act_in[:, 0, :, :].rearrange("p j c -> p (j c)")
                glink(nc.vector.tensor_tensor(a, bank[0][:, :], gath[:, 0, :, :].rearrange("p j c -> p (j c)"),
                                              ALU.add), s, g)
                glink(nc.vector.tensor_tensor(a, a, gath[:, 1, :, :].rearrange("p j c -> p (j c)"), ALU.add), s, g)
                glink(nc.vector.tensor_scalar(a, a, 0.0, None, ALU.max), s, g)
                per_group = TILES * (2 if s == 0 else 1)
                sums_before = g * per_group + (0 if s == 0 else 2 * TILES * GROUPS)
                for j in range(TILES):
                    nc.vector.tensor_scalar(onehot_all[:, :], iota_nodes[:, :], dst_f[:, j:j + 1], None,
                                            ALU.is_equal).then_inc(gen_onehot, 1)
                    n = j * (2 if s == 0 else 1)
                    dve.wait_ge(gen_summed, sums_before + n + 1)
                    for k in range(8):
                        m = msgT[s][:, k * CHUNK:(k + 1) * CHUNK]
                        last = nc.vector.tensor_tensor(m, m, bank[k][:, 0:CHUNK], ALU.add)
                    last.then_inc(gen_added, 1)
                    dve.wait_ge(gen_added, sums_before + n + 1)
                    if s == 0:
                        dve.wait_ge(gen_summed, sums_before + n + 2)
                        for k in range(8):
                            d = deg_one[0:1, k * CHUNK:(k + 1) * CHUNK]
                            last = nc.vector.tensor_tensor(d, d, bank[k][0:1, 0:CHUNK], ALU.add)
                        last.then_inc(gen_added, 1)
                        dve.wait_ge(gen_added, sums_before + n + 2)
                nc.vector.memset(marker[:, :], 0.0).then_inc(gen_group_done, 1)

            links = [0]

            def glink(ins, s, g):
                ins.then_inc(gen_link, 1)
                links[0] = links[0] % 3 + 1
                dve.wait_ge(gen_link, 3 * (s * GROUPS + g) + links[0])

            flag = outside_flag(dve)
            dve.wait_ge(msg_zero, 1 + STEPS)
            for s in range(STEPS):
                with dve.If(flag == 0):
                    windowed_iteration(s, 0, True, False)
                    with dve.Fori(1, LAG) as i:
                        windowed_iteration(s, i, False, False)
                    windowed_iteration(s, LAG, False, True, True)
                    with dve.Fori(LAG + 1, ITERS) as i:
                        windowed_iteration(s, i, False, True)
                    add_gathered(s, s * GROUPS + GROUPS - 1, s * ITERS + ITERS - 1, U - 1, False)
                    for k in range(GROUPS - 3, GROUPS):
                        add_messages(s, k, s * GROUPS + k, k % U, False)
                    for t in TAIL_TILES:
                        update_h(s, t, False)
                with dve.Else():
                    if s == 0:
                        nc.vector.memset(marker[:, :], 0.0).then_inc(gen_group_done, 1)
                    with dve.Fori(0, GROUPS) as g:
                        general_group(s, g)
                    dve.wait_ge(gen_group_done, (s + 1) * GROUPS + 1)
                    nc.vector.memset(marker[:, :], 0.0).then_inc(step_done, 1)
                    update_h(s, 0, s == 0)
                    with dve.Fori(1, NODE_TILES) as t:
                        update_h(s, t, False)


def kernel(x, src, dst, edge_attr_32, L0_gnn_We1, L0_gnn_be1, L0_gnn_We2, L0_gnn_be2, L0_gnn_bias):
    import numpy as np
    import concourse.bacc as bacc
    from concourse.bass_utils import run_bass_kernel_spmd as run

    def padded(a, rows, fill=0):
        a = np.asarray(a)
        return np.concatenate([a, np.full((rows - a.shape[0], *a.shape[1:]), fill, a.dtype)])

    src = padded(src, EP)
    dst = padded(dst, EP, N)
    row = lambda a: np.asarray(a).reshape(1, -1)
    arrays = {
        "x": padded(x, NP),
        "src_groups": np.ascontiguousarray(src.reshape(GROUPS, TILES, P).transpose(2, 0, 1)),
        "dst_groups": np.ascontiguousarray(dst.reshape(GROUPS, TILES, P).transpose(2, 0, 1)),
        "dst_row": row(dst),
        "group_base": row(dst[::EDGE_GROUP].copy()),
        "edge_t": np.ascontiguousarray(padded(edge_attr_32, EP).T),
        "we1": np.asarray(L0_gnn_We1), "be1": row(L0_gnn_be1), "we2": np.asarray(L0_gnn_We2),
        "be2": row(L0_gnn_be2), "bias": row(L0_gnn_bias),
    }
    nc = bacc.Bacc("TRN2", target_bir_lowering=False, num_devices=1)
    args = {k: nc.dram_tensor(k, a.shape, mybir.dt.from_np(a.dtype), kind="ExternalInput").ap()
            for k, a in arrays.items()}
    tables = {k: [nc.dram_tensor(f"{k}{s}", (NP, C), mybir.dt.float32, kind="Internal").ap() for s in range(STEPS)]
              for k in ("p_tab", "q_tab")}
    out = nc.dram_tensor("out", (NP, C), mybir.dt.float32, kind="ExternalOutput").ap()
    gnn_kernel(nc, **args, **tables, out=out)
    return run(nc, [arrays], core_ids=[0]).results[0]["out"][:N]
```

```python
import concourse.bass as bass
from concourse import mybir
from contextlib import ExitStack

N = 3125
E = 53125
C = 128
CE = 32
STEPS = 2
P = 128

NODE_TILES = -(-N // P)
NP = NODE_TILES * P
TILES = 4
EDGE_GROUP = TILES * P
GROUPS = -(-E // EDGE_GROUP)
EP = GROUPS * EDGE_GROUP
WINDOW = 64
U = 4
ITERS = GROUPS // U
LAG = 3
PE_GROUP = U - 1
FETCH = [(u * NODE_TILES // U, (u + 1) * NODE_TILES // U) for u in range(U)]
PARTS = 3
MB = 2
BATCH = 4
NORM_BY_ACT = 1
BATCHES = [(b, min(BATCH, NODE_TILES - b)) for b in range(0, NODE_TILES, BATCH)]
K_PRE = WINDOW + CE + 1
CHUNK = NP // 8
EPS = 1e-5
LOOP_TILES = ITERS - LAG
TAIL_TILES = NODE_TILES - LOOP_TILES
TURNS = LOOP_TILES + 1
assert GROUPS % U == 0 and NP % 8 == 0 and CHUNK <= 512 and TAIL_TILES == 2 and N + WINDOW <= NP


def gnn_kernel(nc, x, src_groups, dst_groups, dst_row, src_row, group_base, edge_t, we1, be1, we2, be2, bias,
               p_tab, q_tab, out):
    fp32, bf16, i32, i16 = mybir.dt.float32, mybir.dt.bfloat16, mybir.dt.int32, mybir.dt.int16
    ALU = mybir.AluOpType
    ACT = mybir.ActivationFunctionType
    AX = mybir.AxisListType

    x_v = x.rearrange("(t p) c -> p t c", p=P)
    p_v = [t.rearrange("(t p) c -> p t c", p=P) for t in p_tab]
    q_v = [t.rearrange("(t p) c -> p t c", p=P) for t in q_tab]

    ctx = ExitStack()
    with ctx:
        def sb(name, shape, dt=fp32):
            return ctx.enter_context(nc.sbuf_tensor(name, shape, dt))

        def sem(name):
            return ctx.enter_context(nc.semaphore(name))

        ident = sb("ident", [P, P])
        ones = sb("ones", [P, 1])
        eps = sb("eps", [P, 1])
        iota_nodes = sb("iota_nodes", [P, NP])
        iota_part = sb("iota_part", [P, 1])
        w1sd = sb("w1sd", [C, 2, C])
        w2 = sb("w2", [C, C])
        tail_rows = sb("tail_rows", [2, C])
        x_sb = sb("x_sb", [P, NODE_TILES, C])
        norm = sb("norm", [P, NODE_TILES, C])
        stage = sb("stage", [P, NODE_TILES, C])
        hT = sb("hT", [C, NP])
        h_tile = sb("h_tile", [C, TAIL_TILES * P])
        tile_out = sb("tile_out", [P, TAIL_TILES, 2, C])
        msgT = [sb(f"msgT{s}", [C, NP]) for s in range(STEPS)]
        deg_one = sb("deg_one", [2, NP])
        stats = sb("stats", [P, NODE_TILES, 6])
        mv = sb("mv", [P, NODE_TILES, 2])
        rstd = sb("rstd", [P, NODE_TILES, 1])
        shift = sb("shift", [P, NODE_TILES, 1])
        dst_pt = sb("dst_pt", [P, GROUPS, TILES], i32)
        rel = sb("rel", [P, GROUPS, TILES])
        base_all = sb("base_all", [P, GROUPS], i32)
        window_node = sb("window_node", [WINDOW, GROUPS])
        first_node = sb("first_node", [P, GROUPS, TILES])
        early = sb("early", [P, GROUPS, TILES])
        extremes = sb("extremes", [P, 4])
        outside = sb("outside", [1, 1], i32)
        lhs = sb("lhs", [K_PRE, U, EDGE_GROUP])
        rhs = sb("rhs", [K_PRE, U, C])
        dst_rows = sb("dst_rows", [WINDOW, U, EDGE_GROUP], i32)
        src_idx = sb("src_idx", [P, U, TILES], i32)
        gath = sb("gath", [P, U, TILES, C])
        act_in = sb("act_in", [P, U, TILES, C])
        onehot = sb("onehot", [P, U, TILES, WINDOW])
        node_ids = sb("node_ids", [P, NODE_TILES, P], i16)
        src_rows = sb("src_rows", [P, P], i32)
        src_rows16 = sb("src_rows16", [P, P], i16)
        src_onehot = sb("src_onehot", [P, NODE_TILES, P], bf16)
        p_parts = [sb(f"p_parts{s}", [P, NODE_TILES, PARTS, C], bf16) for s in range(STEPS)]
        rest = sb("rest", [P, BATCH, C])
        dst_f = sb("dst_f", [P, TILES])
        onehot_all = norm[:, :, :].rearrange("p t c -> p (t c)")
        bank = [ctx.enter_context(nc.psum_tensor(f"bank{b}", [P, 512], fp32)) for b in range(8)]

        x_in = [sem(f"x_in{b}") for b in range(len(BATCHES))]
        w1_in = sem("w1_in")
        weights_in = sem("weights_in")
        tables_in = sem("tables_in")
        ident_zero = sem("ident_zero")
        ident_ready = sem("ident_ready")
        consts_ready = sem("consts_ready")
        deg_ready = sem("deg_ready")
        all_nodes_ready = sem("all_nodes_ready")
        bias_ready = sem("bias_ready")
        msg_zero = sem("msg_zero")
        stats_link = sem("stats_link")
        stats_done = sem("stats_done")
        rstd_ready = sem("rstd_ready")
        std_done = sem("std_done")
        shift_ready = sem("shift_ready")
        norm_done = sem("norm_done")
        act_norm_done = sem("act_norm_done")
        transposed = sem("transposed")
        hT0_done = sem("hT0_done")
        p_prod = sem("p_prod")
        q_prod = sem("q_prod")
        p_staged = sem("p_staged")
        q_staged = sem("q_staged")
        p_stored = [sem(f"p_stored{s}") for s in range(STEPS)]
        q_stored = [sem(f"q_stored{s}") for s in range(STEPS)]
        dve_chain = sem("dve_chain")
        extremes_ready = sem("extremes_ready")
        outside_sum = sem("outside_sum")
        outside_ready = sem("outside_ready")
        dstrow_in = [sem(f"dstrow_in{u}") for u in range(U)]
        window_in = [sem(f"window_in{u}") for u in range(U)]
        idx_in = [sem(f"idx_in{u}") for u in range(U)]
        groups_started = sem("groups_started")
        ids_ready = sem("ids_ready")
        srcrow_in = sem("srcrow_in")
        src16_ready = sem("src16_ready")
        src_onehot_ready = sem("src_onehot_ready")
        rows_fetched = sem("rows_fetched")
        rows_joined = sem("rows_joined")
        first_parts = sem("first_parts")
        parts_ready = sem("parts_ready")
        gathered = [sem(f"gathered{u}") for u in range(U)]
        picks_built = sem("picks_built")
        sum_onehot_built = sem("sum_onehot_built")
        pre_done = sem("pre_done")
        sum_done = sem("sum_done")
        relu_done = sem("relu_done")
        msgs_summed = sem("msgs_summed")
        msgs_added = sem("msgs_added")
        gen_link = sem("gen_link")
        gen_in = sem("gen_in")
        gen_gathered = sem("gen_gathered")
        gen_pre = sem("gen_pre")
        gen_onehot = sem("gen_onehot")
        gen_summed = sem("gen_summed")
        gen_added = sem("gen_added")
        gen_group_done = sem("gen_group_done")
        step_done = sem("step_done")
        update_prod = sem("update_prod")
        updated = sem("updated")
        h_kept = sem("h_kept")
        split_link = sem("split_link")
        tile_prod = sem("tile_prod")
        tile_staged = sem("tile_staged")
        stored = sem("stored")
        marker = sb("marker", [1, 1])

        TABLE_DMAS = [len(BATCHES)] + [TURNS] * (STEPS - 1)
        W_DMAS, T_DMAS = 3 + 2 * U, 2

        block = ctx.enter_context(nc.Block())

        by_dma = [TILES - (u == PE_GROUP) for u in range(U)]
        fetched = bank[7][:, 0:PARTS * C]

        def dve_share(n):
            return n - NORM_BY_ACT if n == BATCH else n

        def rows_before(s, i, u):
            return by_dma[u] * (s * ITERS + i)

        def outside_flag(eng):
            eng.wait_ge(outside_ready, 1)
            return eng.value_load(outside[0:1, 0:1], min_val=0, max_val=1)

        @block.sync
        def _(sp):
            def load_x(b, t0, n):
                sp.dma_start(x_sb[:, t0:t0 + n, :], x_v[:, t0:t0 + n, :]).then_inc(x_in[b], 16)

            load_x(0, *BATCHES[0])
            sp.dma_start(dst_pt[:, :, :], dst_groups).then_inc(tables_in, 16)
            sp.dma_start(base_all[:, :], group_base.to_broadcast([P, GROUPS])).then_inc(tables_in, 16)
            load_x(1, *BATCHES[1])
            sp.dma_start(w1sd[:, :, :], we1[0:2 * C, :].rearrange("(k p) c -> p k c", k=2)).then_inc(w1_in, 16)
            for b in range(2, len(BATCHES)):
                load_x(b, *BATCHES[b])
            for u in range(U):
                sp.dma_start(rhs[WINDOW:WINDOW + CE, u, :], we1[2 * C:2 * C + CE, :]).then_inc(weights_in, 16)
                sp.dma_start(rhs[WINDOW + CE:K_PRE, u, :], be1).then_inc(weights_in, 16)
            sp.dma_start(w2[:, :], we2).then_inc(weights_in, 16)
            sp.dma_start(tail_rows[0:1, :], be2).then_inc(weights_in, 16)
            sp.dma_start(tail_rows[1:2, :], bias).then_inc(weights_in, 16)

            def load_group(s, i, u, first):
                k = i * U + u
                done = s * GROUPS + k
                if not first:
                    sp.wait_ge(gathered[u], 16 * rows_before(s, i, u))
                sp.dma_start(src_idx[:, u, :], src_groups[:, bass.ds(k, 1), :].rearrange("p g j -> p (g j)")
                             ).then_inc(idx_in[u], 16)
                if not first:
                    sp.wait_ge(picks_built, done - U + 1)
                sp.dma_start(dst_rows[:, u, :],
                             dst_row[0:1, bass.ds(k * EDGE_GROUP, EDGE_GROUP)].to_broadcast([WINDOW, EDGE_GROUP])
                             ).then_inc(dstrow_in[u], 16)
                if not first:
                    sp.wait_ge(pre_done, done - U + 1)
                sp.dma_start(lhs[WINDOW:WINDOW + CE, u, :], edge_t[:, bass.ds(k * EDGE_GROUP, EDGE_GROUP)]
                             ).then_inc(window_in[u], 16)

            def load_src_row(s, i, first):
                if not first:
                    sp.wait_ge(src16_ready, s * ITERS + i)
                end = (PE_GROUP + 1) * EDGE_GROUP
                sp.dma_start(src_rows[:, :], src_row[bass.ds(i, 1), end - P:end].to_broadcast([P, P])
                             ).then_inc(srcrow_in, 16)

            def load_window(s, i, u):
                base = sp.value_load(base_all[0:1, bass.ds(i * U + u, 1)], min_val=0, max_val=N)
                sp.dma_start(rhs[0:WINDOW, u, :], q_tab[s][bass.ds(base, WINDOW), :]).then_inc(window_in[u], 16)

            def general_group(s, g):
                seq = s * GROUPS + g
                sp.wait_ge(gen_group_done, seq + 1)
                sp.dma_start(src_idx[:, 0, :], src_groups[:, bass.ds(g, 1), :].rearrange("p g j -> p (g j)")
                             ).then_inc(gen_in, 16)
                sp.dma_start(src_idx[:, 1, :], dst_groups[:, bass.ds(g, 1), :].rearrange("p g j -> p (g j)")
                             ).then_inc(gen_in, 16)
                sp.dma_start(lhs[WINDOW:WINDOW + CE, 0, :], edge_t[:, bass.ds(g * EDGE_GROUP, EDGE_GROUP)]
                             ).then_inc(gen_in, 16)

            for b, (t0, n) in enumerate(BATCHES):
                sp.wait_ge(p_staged, b + 1)
                sp.dma_start(p_v[0][:, t0:t0 + n, :], stage[:, t0:t0 + n, :]).then_inc(p_stored[0], 16)
            flag = outside_flag(sp)
            for s in range(STEPS):
                with sp.If(flag == 0):
                    load_src_row(s, 0, s == 0)
                    for u in range(U):
                        load_group(s, 0, u, s == 0)
                    sp.wait_ge(q_stored[s], 16 * TABLE_DMAS[s])
                    for u in range(U):
                        load_window(s, 0, u)
                    with sp.Fori(1, ITERS) as i:
                        load_src_row(s, i, False)
                        for u in range(U):
                            load_group(s, i, u, False)
                            load_window(s, i, u)
                with sp.Else():
                    with sp.Fori(0, GROUPS) as g:
                        general_group(s, g)

        @block.gpsimd
        def _(pool):
            nc.gpsimd.memset(ident[:, :], 0.0).then_inc(ident_zero, 1)
            pool.wait_ge(ident_zero, 1)
            nc.gpsimd.affine_select(out=ident[:, :], in_=ident[:, :], compare_op=ALU.not_equal, fill=1.0, base=0,
                                    pattern=[[-1, P]], channel_multiplier=1).then_inc(ident_ready, 1)
            nc.gpsimd.iota(iota_part[:, :], pattern=[[0, 1]], base=0, channel_multiplier=1,
                           allow_small_or_imprecise_dtypes=True)
            nc.gpsimd.iota(iota_nodes[:, 0:WINDOW], pattern=[[1, WINDOW]], base=0, channel_multiplier=0,
                           allow_small_or_imprecise_dtypes=True)
            nc.gpsimd.memset(eps[:, :], EPS)
            nc.gpsimd.memset(ones[:, :], 1.0).then_inc(consts_ready, 1)
            pool.wait_ge(consts_ready, 1)
            nc.gpsimd.iota(first_node[:, :, :].rearrange("p (i u) j -> p i (u j)", u=U), pattern=[[P, ITERS], [0, U * TILES]],
                           base=-(LAG - 1) * P, channel_multiplier=0, allow_small_or_imprecise_dtypes=True
                           ).then_inc(ids_ready, 1)
            pool.wait_ge(ids_ready, 1)
            nc.gpsimd.memset(lhs[WINDOW + CE:K_PRE, :, :], 1.0).then_inc(bias_ready, 1)
            pool.wait_ge(bias_ready, 1)
            nc.gpsimd.iota(node_ids[:, :, :], pattern=[[P, NODE_TILES], [0, P]], base=0, channel_multiplier=1,
                           allow_small_or_imprecise_dtypes=True).then_inc(ids_ready, 1)
            for s in range(STEPS):
                nc.gpsimd.memset(msgT[s][:, :], 0.0).then_inc(msg_zero, 1)

            def windowed_group(s, i, u, first):
                if not first:
                    pool.wait_ge(sum_done, s * GROUPS + i * U + u - U + 1)
                pool.wait_ge(idx_in[u], 16 * (s * ITERS + i + 1))
                pool.sem_inc(groups_started, 1)
                for j in range(by_dma[u]):
                    nc.gpsimd.indirect_dma_start(gath[:, u, j, :], None, p_tab[s],
                                                 bass.IndirectOffsetOnAxis(ap=src_idx[:, u, j:j + 1], axis=0)
                                                 ).then_inc(gathered[u], 16)

            def general_group(s, g):
                seq = s * GROUPS + g
                pool.wait_ge(gen_in, 48 * (seq + 1))
                pool.sem_inc(groups_started, 1)
                for k, tab in enumerate((p_tab[s], q_tab[s])):
                    for j in range(TILES):
                        nc.gpsimd.indirect_dma_start(gath[:, k, j, :], None, tab,
                                                     bass.IndirectOffsetOnAxis(ap=src_idx[:, k, j:j + 1], axis=0)
                                                     ).then_inc(gen_gathered, 16)

            flag = outside_flag(pool)
            for s in range(STEPS):
                pool.wait_ge(p_stored[s], 16 * TABLE_DMAS[s])
                with pool.If(flag == 0):
                    for u in range(U):
                        windowed_group(s, 0, u, s == 0)
                    with pool.Fori(1, ITERS) as i:
                        for u in range(U):
                            windowed_group(s, i, u, False)
                with pool.Else():
                    pool.wait_ge(q_stored[s], 16 * TABLE_DMAS[s])
                    if s == 0:
                        nc.gpsimd.iota(iota_nodes[:, :], pattern=[[1, NP]], base=0, channel_multiplier=0,
                                       allow_small_or_imprecise_dtypes=True).then_inc(all_nodes_ready, 1)
                    with pool.Fori(0, GROUPS) as g:
                        general_group(s, g)

        @block.scalar
        def _(act):
            def stage_table(b, t0, n, banks, prod, staged, to):
                act.wait_ge(prod, b + 1)
                nc.scalar.activation(to[:, t0:t0 + n, :],
                                     bank[banks + b % 2][:, 0:n * C].rearrange("p (t c) -> p t c", c=C), ACT.Copy
                                     ).then_inc(staged, 1)

            def store_q(b, t0, n):
                act.wait_ge(q_staged, b + 1)
                act.dma_start(q_v[0][:, t0:t0 + n, :], norm[:, t0:t0 + n, :]).then_inc(q_stored[0], 16)

            def part_first(t0, n):
                nc.scalar.activation(p_parts[0][:, t0:t0 + n, 0, :], stage[:, t0:t0 + n, :], ACT.Copy
                                     ).then_inc(first_parts, 1)

            def normalize(b, t0, n):
                if dve_share(n) < n:
                    act.wait_ge(shift_ready, b + 1)
                    for t in range(t0 + dve_share(n), t0 + n):
                        last = nc.scalar.activation(norm[:, t, :], x_sb[:, t, :], ACT.Identity, bias=shift[:, t, :],
                                                    scale=rstd[:, t, :])
                    last.then_inc(act_norm_done, 1)

            def root(b, t0, n):
                act.wait_ge(stats_done, b + 1)
                nc.scalar.activation(rstd[:, t0:t0 + n, :], mv[:, t0:t0 + n, 1:2], ACT.Sqrt, bias=eps[:, :]
                                     ).then_inc(std_done, 1)

            root(0, *BATCHES[0])
            root(1, *BATCHES[1])
            normalize(0, *BATCHES[0])
            for b, (t0, n) in enumerate(BATCHES):
                if b + 2 < len(BATCHES):
                    root(b + 2, *BATCHES[b + 2])
                if b + 1 < len(BATCHES):
                    normalize(b + 1, *BATCHES[b + 1])
                act.wait_ge(transposed, b + 1)
                nc.scalar.activation(hT[:, t0 * P:(t0 + n) * P], bank[4 + b % 2][:, 0:n * P], ACT.Relu
                                     ).then_inc(hT0_done, 1)
                if b >= 1:
                    stage_table(b - 1, *BATCHES[b - 1], 0, p_prod, p_staged, stage)
            stage_table(len(BATCHES) - 1, *BATCHES[-1], 0, p_prod, p_staged, stage)
            act.wait_ge(p_staged, len(BATCHES))
            part_first(*BATCHES[0])
            part_first(*BATCHES[1])
            for b, (t0, n) in enumerate(BATCHES):
                stage_table(b, t0, n, 2, q_prod, q_staged, norm)
                if b >= 1:
                    store_q(b - 1, *BATCHES[b - 1])
                if b + 2 < len(BATCHES):
                    part_first(*BATCHES[b + 2])
            store_q(len(BATCHES) - 1, *BATCHES[-1])
            nc.scalar.activation(deg_one[:, :], iota_part[0:2, :].to_broadcast([2, NP]), ACT.Copy).then_inc(deg_ready, 1)

            def relu_group(s, i, u):
                act.wait_ge(sum_done, s * GROUPS + i * U + u + 1)
                nc.scalar.activation(act_in[:, u, :, :], act_in[:, u, :, :], ACT.Relu).then_inc(relu_done, 1)

            def send_tiles(s, t, first, n=1, split=False):
                seq = s * TURNS + t
                act.wait_ge(tile_prod, seq + 1)
                rows = bass.ds(t * P, n * P)
                if s < STEPS - 1:
                    if not first:
                        act.wait_ge(p_stored[s + 1], 16 * t)
                        act.wait_ge(q_stored[s + 1], 16 * t)
                        if split:
                            act.wait_ge(parts_ready, len(BATCHES) + t)
                    nc.scalar.activation(tile_out[:, 0:n, :, :], bank[6][:, 0:n * 2 * C].rearrange(
                        "p (t k c) -> p t k c", t=n, k=2), ACT.Copy).then_inc(tile_staged, 1)
                    act.wait_ge(tile_staged, seq + 1)
                    for k, (tab, is_stored) in enumerate(((p_tab, p_stored), (q_tab, q_stored))):
                        act.dma_start(tab[s + 1][rows, :].rearrange("(t p) c -> p t c", t=n), tile_out[:, 0:n, k, :]
                                      ).then_inc(is_stored[s + 1], 16)
                    if split:
                        nc.scalar.activation(p_parts[s + 1][:, bass.ds(t, n), 0, :], tile_out[:, 0:n, 0, :], ACT.Copy
                                             ).then_inc(first_parts, 1)
                else:
                    if not first:
                        act.wait_ge(stored, 16 * t)
                    nc.scalar.activation(tile_out[:, 0:n, 0, :], bank[6][:, 0:n * C].rearrange(
                        "p (t c) -> p t c", t=n), ACT.Copy).then_inc(tile_staged, 1)
                    act.wait_ge(tile_staged, seq + 1)
                    act.dma_start(out[rows, :].rearrange("(t p) c -> p t c", t=n), tile_out[:, 0:n, 0, :]
                                  ).then_inc(stored, 16)

            def narrow_src_row(s, i, first):
                turn = s * ITERS + i
                act.wait_ge(srcrow_in, 16 * (turn + 1))
                if not first:
                    act.wait_ge(src_onehot_ready, U * turn)
                nc.scalar.activation(src_rows16[:, :], src_rows[:, :], ACT.Copy).then_inc(src16_ready, 1)

            def windowed_iteration(s, i, tile, first_tile=False, last=False):
                for u in range(U):
                    if u == U - 1 and tile and not last:
                        send_tiles(s, i - LAG, first_tile, split=True)
                    if u == U - 2 and not last:
                        narrow_src_row(s, i + 1, False)
                    if u == U - 2 and last and s < STEPS - 1:
                        narrow_src_row(s + 1, 0, False)
                    relu_group(s, i, u)
                if last:
                    send_tiles(s, i - LAG, False, split=True)

            flag = outside_flag(act)
            for s in range(STEPS):
                with act.If(flag == 0):
                    if s == 0:
                        narrow_src_row(0, 0, True)
                    with act.Fori(0, LAG) as i:
                        windowed_iteration(s, i, False)
                    windowed_iteration(s, LAG, True, True)
                    with act.Fori(LAG + 1, ITERS - 1) as i:
                        windowed_iteration(s, i, True)
                    windowed_iteration(s, ITERS - 1, True, last=True)
                    send_tiles(s, LOOP_TILES, False, TAIL_TILES, split=True)
                with act.Else():
                    send_tiles(s, 0, True)
                    with act.Fori(1, LOOP_TILES) as t:
                        send_tiles(s, t, False)
                    send_tiles(s, LOOP_TILES, False, TAIL_TILES)
                if s < STEPS - 1:
                    act.wait_ge(p_stored[s + 1], 16 * TURNS)
                    act.wait_ge(q_stored[s + 1], 16 * TURNS)
            act.wait_ge(stored, 16 * TURNS)

        @block.tensor
        def _(pe):
            pe.wait_ge(ident_ready, 1)
            pe.wait_ge(consts_ready, 1)

            def project(which, b, t0, n, prod, staged):
                if b >= 2:
                    pe.wait_ge(staged, b - 1)
                for j in range(n):
                    t = t0 + j
                    last = nc.tensor.matmul(bank[2 * which + b % 2][:, j * C:(j + 1) * C],
                                            hT[:, t * P:(t + 1) * P], w1sd[:, which, :], start=True, stop=True)
                last.then_inc(prod, 1)

            def transpose(b, t0, n):
                pe.wait_ge(norm_done, b + 1)
                if dve_share(n) < n:
                    pe.wait_ge(act_norm_done, b + 1)
                if b >= 2:
                    pe.wait_ge(hT0_done, b - 1)
                for j in range(n):
                    last = nc.tensor.transpose(bank[4 + b % 2][:, j * P:(j + 1) * P], norm[:, t0 + j, :], ident[:, :])
                last.then_inc(transposed, 1)

            for b, (t0, n) in enumerate(BATCHES):
                transpose(b, t0, n)
                if b == 1:
                    pe.wait_ge(w1_in, 16)
                if b >= 1:
                    pe.wait_ge(hT0_done, b)
                    project(0, b - 1, *BATCHES[b - 1], p_prod, p_staged)
            pe.wait_ge(hT0_done, len(BATCHES))
            project(0, len(BATCHES) - 1, *BATCHES[-1], p_prod, p_staged)
            pe.wait_ge(extremes_ready, 1)
            nc.tensor.matmul(bank[7][0:1, 0:1], extremes[:, 3:4], ones[:, :], start=True, stop=True
                             ).then_inc(outside_sum, 1)
            for b, (t0, n) in enumerate(BATCHES):
                project(1, b, t0, n, q_prod, q_staged)

            def pre_activation(s, i, u, first):
                done = s * GROUPS + i * U + u
                pe.wait_ge(window_in[u], 32 * (s * ITERS + i + 1))
                pe.wait_ge(picks_built, done + 1)
                if not first:
                    pe.wait_ge(sum_done, done - U + 1)
                for j in range(TILES):
                    last = nc.tensor.matmul(bank[u][:, j * C:(j + 1) * C], lhs[:, u, j * P:(j + 1) * P], rhs[:, u, :],
                                            start=True, stop=True)
                last.then_inc(pre_done, 1)

            def fetch_rows(s, i, u, first):
                pe.wait_ge(src_onehot_ready, U * (s * ITERS + i) + u + 1)
                if u == 0 and not first:
                    pe.wait_ge(rows_joined, s * ITERS + i)
                for t in range(*FETCH[u]):
                    last = nc.tensor.matmul(fetched, src_onehot[:, t, :],
                                            p_parts[s][:, t, :, :].rearrange("p k c -> p (k c)"),
                                            start=(t == 0), stop=(t == NODE_TILES - 1))
                last.then_inc(rows_fetched, 1)

            def sum_messages(s, seq, u, first):
                pe.wait_ge(sum_onehot_built, seq + 1)
                pe.wait_ge(relu_done, seq + 1)
                if not first:
                    pe.wait_ge(msgs_added, seq - MB + 1)
                m = bank[4 + u % MB]
                for j in range(TILES):
                    last = nc.tensor.matmul(m[:, 0:WINDOW], act_in[:, u, j, :], onehot[:, u, j, :],
                                            start=(j == 0), stop=(j == TILES - 1))
                if s == 0:
                    for j in range(TILES):
                        half = onehot[:, u, j, :].bitcast(bf16).rearrange("p (n two) -> p n two", two=2)[:, :, 1]
                        last = nc.tensor.matmul(m[0:1, WINDOW:2 * WINDOW],
                                                ones[:, :].bitcast(bf16)[:, 1:2], half,
                                                start=(j == 0), stop=(j == TILES - 1))
                last.then_inc(msgs_summed, 1)

            def update_tiles(s, t, first, n=1):
                nodes = bass.ds(t * P, n * P)
                if not first:
                    pe.wait_ge(tile_staged, s * TURNS + t)
                rows = 1 if s < STEPS - 1 else 2
                nc.tensor.matmul(bank[6][:, 0:n * P], w2[:, :], msgT[s][:, nodes], start=True, stop=False)
                nc.tensor.matmul(bank[6][:, 0:n * P], tail_rows[0:rows, :], deg_one[0:rows, nodes],
                                 start=False, stop=True).then_inc(update_prod, 1)

            def finish_tiles(s, t, n=1):
                seq = s * TURNS + t
                pe.wait_ge(updated, seq + 1)
                for j in range(n):
                    h = h_tile[:, j * P:(j + 1) * P]
                    if s < STEPS - 1:
                        last = nc.tensor.matmul(bank[6][:, j * 2 * C:(j + 1) * 2 * C], h,
                                                w1sd[:, :, :].rearrange("p k c -> p (k c)"), start=True, stop=True)
                    else:
                        o = bank[6][:, j * C:(j + 1) * C]
                        nc.tensor.matmul(o, h, ident[:, :], start=True, stop=False)
                        last = nc.tensor.matmul(o, ident[:, :],
                                                x_sb[:, bass.ds(t + j, 1), :].rearrange("p t c -> p (t c)"),
                                                start=False, stop=True)
                last.then_inc(tile_prod, 1)

            def windowed_iteration(s, i, first, tile, first_tile=False):
                for u in range(U):
                    if u == U - 1 and tile:
                        pe.wait_ge(msgs_added, s * GROUPS + i * U)
                        update_tiles(s, i - LAG, first_tile and s == 0)
                    pre_activation(s, i, u, first and s == 0)
                    if not (first and s > 0):
                        fetch_rows(s, i, u, first)
                    if u >= 2 or not first:
                        seq = s * GROUPS + i * U + u - 2
                        sum_messages(s, seq, (u - 2) % U, first and s == 0 and u - 2 < MB)
                if tile:
                    finish_tiles(s, i - LAG)

            def general_group(s, g):
                seq = s * GROUPS + g
                pe.wait_ge(gen_in, 48 * (seq + 1))
                for j in range(TILES):
                    last = nc.tensor.matmul(bank[0][:, j * C:(j + 1) * C],
                                            lhs[WINDOW:K_PRE, 0, j * P:(j + 1) * P],
                                            rhs[WINDOW:K_PRE, 0, :], start=True, stop=True)
                last.then_inc(gen_pre, 1)
                per_group = TILES * (2 if s == 0 else 1)
                sums_before = g * per_group + (0 if s == 0 else 2 * TILES * GROUPS)
                for j in range(TILES):
                    pe.wait_ge(gen_onehot, seq * TILES + j + 1)
                    for k in range(8):
                        last = nc.tensor.matmul(bank[k][:, 0:CHUNK], act_in[:, 0, j, :],
                                                onehot_all[:, k * CHUNK:(k + 1) * CHUNK], start=True, stop=True)
                    last.then_inc(gen_summed, 1)
                    if s == 0:
                        pe.wait_ge(gen_added, sums_before + 2 * j + 1)
                        for k in range(8):
                            last = nc.tensor.matmul(bank[k][0:1, 0:CHUNK], ones[:, :],
                                                    onehot_all[:, k * CHUNK:(k + 1) * CHUNK], start=True, stop=True)
                        last.then_inc(gen_summed, 1)

            flag = outside_flag(pe)
            pe.wait_ge(bias_ready, 1)
            pe.wait_ge(weights_in, 16 * W_DMAS)
            pe.wait_ge(p_staged, len(BATCHES))
            pe.wait_ge(q_staged, len(BATCHES))
            for s in range(STEPS):
                with pe.If(flag == 0):
                    pe.wait_ge(parts_ready, len(BATCHES) + s * TURNS)
                    if s > 0:
                        for u in range(U):
                            fetch_rows(s, 0, u, False)
                    windowed_iteration(s, 0, True, False)
                    with pe.Fori(1, LAG) as i:
                        windowed_iteration(s, i, False, False)
                    windowed_iteration(s, LAG, False, True, True)
                    with pe.Fori(LAG + 1, ITERS) as i:
                        windowed_iteration(s, i, False, True)
                    for k in (GROUPS - 2, GROUPS - 1):
                        sum_messages(s, s * GROUPS + k, k % U, False)
                    pe.wait_ge(msgs_added, (s + 1) * GROUPS)
                with pe.Else():
                    with pe.Fori(0, GROUPS) as g:
                        general_group(s, g)
                    pe.wait_ge(step_done, s + 1)
                    update_tiles(s, 0, s == 0)
                    finish_tiles(s, 0)
                    with pe.Fori(1, LOOP_TILES) as t:
                        update_tiles(s, t, False)
                        finish_tiles(s, t)
                update_tiles(s, LOOP_TILES, False, TAIL_TILES)
                finish_tiles(s, LOOP_TILES, TAIL_TILES)

        @block.vector
        def _(dve):
            chain = [0]

            def link(ins):
                chain[0] += 1
                ins.then_inc(dve_chain, 1)
                dve.wait_ge(dve_chain, chain[0])

            def tile_stats(b, t0, n):
                dve.wait_ge(x_in[b], 16)
                for t in range(t0, t0 + n):
                    last = nc.vector.bn_stats(stats[:, t, :], x_sb[:, t, :])
                last.then_inc(stats_link, 1)

            def tile_variance(b, t0, n):
                dve.wait_ge(stats_link, b + 1)
                for t in range(t0, t0 + n):
                    last = nc.vector.bn_aggr(mv[:, t, :], stats[:, t, :])
                last.then_inc(stats_done, 1)

            def invert_std(b, t0, n):
                dve.wait_ge(std_done, b + 1)
                nc.vector.reciprocal(rstd[:, t0:t0 + n, :], rstd[:, t0:t0 + n, :]).then_inc(rstd_ready, 1)

            def normalize(b, t0, n):
                dve.wait_ge(stats_done, b + 1)
                dve.wait_ge(rstd_ready, b + 1)
                by_dve = dve_share(n)
                if by_dve < n:
                    nc.vector.scalar_tensor_tensor(shift[:, t0 + by_dve:t0 + n, :], mv[:, t0 + by_dve:t0 + n, 0:1], -1.0,
                                                   rstd[:, t0 + by_dve:t0 + n, :], ALU.mult, ALU.mult
                                                   ).then_inc(shift_ready, 1)
                for t in range(t0, t0 + by_dve):
                    last = nc.vector.tensor_scalar(norm[:, t, :], x_sb[:, t, :], mv[:, t, 0:1], rstd[:, t, :],
                                                   ALU.subtract, ALU.mult)
                last.then_inc(norm_done, 1)

            def check_edges():
                flat = lambda a: a[:, :, :].rearrange("p g j -> p (g j)")
                dve.wait_ge(tables_in, 16 * T_DMAS)
                dve.wait_ge(ids_ready, 1)
                nc.vector.tensor_tensor(rel[:, :, :], dst_pt[:, :, :],
                                        base_all[:, :].unsqueeze(2).to_broadcast([P, GROUPS, TILES]), ALU.subtract)
                nc.vector.tensor_scalar(window_node[:, :], base_all[0:WINDOW, :], iota_part[0:WINDOW, :], None,
                                        ALU.add)
                link(nc.vector.tensor_tensor(flat(early), flat(dst_pt), flat(first_node), ALU.is_lt))
                nc.vector.tensor_reduce(extremes[:, 0:1], flat(rel), AX.X, ALU.max)
                nc.vector.tensor_reduce(extremes[:, 1:2], flat(rel), AX.X, ALU.min)
                link(nc.vector.tensor_reduce(extremes[:, 2:3], flat(early), AX.X, ALU.max))
                link(nc.vector.scalar_tensor_tensor(extremes[:, 2:3], extremes[:, 1:2], 0.0, extremes[:, 2:3],
                                                    ALU.is_lt, ALU.add))
                nc.vector.scalar_tensor_tensor(extremes[:, 3:4], extremes[:, 0:1], float(WINDOW - 1),
                                               extremes[:, 2:3], ALU.is_gt, ALU.add).then_inc(extremes_ready, 1)

            tile_stats(0, *BATCHES[0])
            dve.wait_ge(consts_ready, 1)
            tile_variance(0, *BATCHES[0])
            for b, (t0, n) in enumerate(BATCHES):
                ahead = b + 1 < len(BATCHES)
                if ahead:
                    tile_stats(b + 1, *BATCHES[b + 1])
                invert_std(b, t0, n)
                if ahead:
                    tile_variance(b + 1, *BATCHES[b + 1])
                normalize(b, t0, n)
            check_edges()
            dve.wait_ge(outside_sum, 1)
            nc.vector.tensor_scalar(outside[:, :], bank[7][0:1, 0:1], 1.0, None, ALU.min).then_inc(outside_ready, 1)

            def split(parts, src, seq):
                n = src.shape[1]
                r = rest[:, 0:n, :]
                out = [parts[:, :, k, :] for k in range(PARTS)]
                nc.vector.tensor_tensor(r, src, out[0], ALU.subtract).then_inc(split_link, 1)
                dve.wait_ge(split_link, 2 * seq + 1)
                nc.vector.tensor_scalar(out[1], r, 1.0, None, ALU.mult).then_inc(split_link, 1)
                dve.wait_ge(split_link, 2 * seq + 2)
                nc.vector.tensor_tensor(out[2], r, out[1], ALU.subtract).then_inc(parts_ready, 1)

            def split_tiles(s, t, n=1):
                dve.wait_ge(first_parts, len(BATCHES) + t + 1)
                dve.wait_ge(parts_ready, len(BATCHES) + t)
                split(p_parts[s + 1][:, bass.ds(t, n), :, :], tile_out[:, 0:n, 0, :],
                      len(BATCHES) + t)

            def build_src_onehot(s, i, u):
                if u == 0:
                    dve.wait_ge(src16_ready, s * ITERS + i + 1)
                t0, t1 = FETCH[u]
                nc.vector.tensor_tensor(src_onehot[:, t0:t1, :],
                                        src_rows16[:, :].unsqueeze(1).to_broadcast([P, t1 - t0, P]),
                                        node_ids[:, t0:t1, :], ALU.is_equal).then_inc(src_onehot_ready, 1)

            def join_rows(s, i):
                dve.wait_ge(rows_fetched, U * (s * ITERS + i + 1))
                nc.vector.tensor_reduce(gath[:, PE_GROUP, TILES - 1, :], fetched.rearrange("p (k c) -> p c k", k=PARTS),
                                        AX.X, ALU.add).then_inc(rows_joined, 1)
                dve.wait_ge(rows_joined, s * ITERS + i + 1)

            def build_picks(s, i, u, first):
                k = i * U + u
                done = s * GROUPS + k
                dve.wait_ge(dstrow_in[u], 16 * (s * ITERS + i + 1))
                if not first:
                    dve.wait_ge(pre_done, done - U + 1)
                nc.vector.tensor_scalar(lhs[0:WINDOW, u, :], dst_rows[:, u, :],
                                        window_node[:, bass.ds(k, 1)], None, ALU.is_equal).then_inc(picks_built, 1)

            def build_sum_onehot(s, i, u, first):
                k = i * U + u
                if not first:
                    dve.wait_ge(msgs_summed, s * GROUPS + k - U + 1)
                nc.vector.tensor_tensor(onehot[:, u, :, :],
                                        rel[:, bass.ds(k, 1), :].rearrange("p g j -> p (g j)").unsqueeze(2)
                                        .to_broadcast([P, TILES, WINDOW]),
                                        iota_nodes[:, 0:WINDOW].unsqueeze(1).to_broadcast([P, TILES, WINDOW]),
                                        ALU.is_equal).then_inc(sum_onehot_built, 1)

            def add_gathered(s, seq, it, u, first):
                dve.wait_ge(pre_done, seq + 1)
                dve.wait_ge(gathered[u], 16 * it)
                if not first:
                    dve.wait_ge(msgs_summed, seq - U + 2)
                nc.vector.tensor_tensor(act_in[:, u, :, :].rearrange("p j c -> p (j c)"), bank[u][:, :],
                                        gath[:, u, :, :].rearrange("p j c -> p (j c)"), ALU.add
                                        ).then_inc(sum_done, 1)

            def window_base(k):
                return dve.value_load(base_all[0:1, bass.ds(k, 1)], min_val=0, max_val=N)

            def add_messages(s, base, seq, u, first):
                dve.wait_ge(msgs_summed, seq + 1)
                if not first:
                    dve.wait_ge(msgs_added, seq)
                if s == 0:
                    nc.vector.tensor_tensor(deg_one[0:1, bass.ds(base, WINDOW)], deg_one[0:1, bass.ds(base, WINDOW)],
                                            bank[4 + u % MB][0:1, WINDOW:2 * WINDOW], ALU.add)
                nc.vector.tensor_tensor(msgT[s][:, bass.ds(base, WINDOW)], msgT[s][:, bass.ds(base, WINDOW)],
                                        bank[4 + u % MB][:, 0:WINDOW], ALU.add).then_inc(msgs_added, 1)

            def update_h(s, t, first, n=1):
                seq = s * TURNS + t
                nodes = bass.ds(t * P, n * P)
                h = h_tile[:, 0:n * P]
                dve.wait_ge(update_prod, seq + 1)
                if not first:
                    dve.wait_ge(tile_prod, seq)
                    dve.wait_ge(h_kept, seq if s == 0 else TURNS)
                nc.vector.tensor_tensor(h, hT[:, nodes], bank[6][:, 0:n * P], ALU.add).then_inc(updated, 1)
                if s < STEPS - 1:
                    dve.wait_ge(updated, seq + 1)
                    nc.vector.tensor_scalar(hT[:, nodes], h, 1.0, None, ALU.mult).then_inc(h_kept, 1)

            def windowed_iteration(s, i, first, tile, first_tile=False, last=False):
                for u in range(U):
                    if u < U - 1 or not last:
                        ahead = u + 1
                        build_picks(s, i + ahead // U, ahead % U, first and s == 0 and ahead < U)
                    build_sum_onehot(s, i, u, first and s == 0)
                    if u == U - 1 and tile and not first_tile and s < STEPS - 1:
                        split_tiles(s, i - LAG - 1)
                    if u >= 1 or not first:
                        seq = s * GROUPS + i * U + u - 1
                        it = rows_before(s, i + (u >= 1), (u - 1) % U)
                        if u == PE_GROUP:
                            join_rows(s, i)
                        add_gathered(s, seq, it, (u - 1) % U, first and s == 0)
                    if u < U - 1 and not (first and s > 0):
                        build_src_onehot(s, i, u + 1)
                    if u == U - 1 and not last:
                        build_src_onehot(s, i + 1, 0)
                    if u >= 3 or not first:
                        k = i * U + u - 3
                        add_messages(s, window_base(k), s * GROUPS + k, (u - 3) % U, first and s == 0 and u == 3)
                if tile:
                    update_h(s, i - LAG, first_tile and s == 0)

            def general_group(s, g):
                seq = s * GROUPS + g
                dve.wait_ge(gen_pre, seq + 1)
                dve.wait_ge(gen_gathered, 2 * TILES * 16 * (seq + 1))
                nc.vector.tensor_copy(dst_f[:, :], src_idx[:, 1, :])
                a = act_in[:, 0, :, :].rearrange("p j c -> p (j c)")
                glink(nc.vector.tensor_tensor(a, bank[0][:, :], gath[:, 0, :, :].rearrange("p j c -> p (j c)"),
                                              ALU.add), s, g)
                glink(nc.vector.tensor_tensor(a, a, gath[:, 1, :, :].rearrange("p j c -> p (j c)"), ALU.add), s, g)
                glink(nc.vector.tensor_scalar(a, a, 0.0, None, ALU.max), s, g)
                per_group = TILES * (2 if s == 0 else 1)
                sums_before = g * per_group + (0 if s == 0 else 2 * TILES * GROUPS)
                for j in range(TILES):
                    nc.vector.tensor_scalar(onehot_all[:, :], iota_nodes[:, :], dst_f[:, j:j + 1], None,
                                            ALU.is_equal).then_inc(gen_onehot, 1)
                    n = j * (2 if s == 0 else 1)
                    dve.wait_ge(gen_summed, sums_before + n + 1)
                    for k in range(8):
                        m = msgT[s][:, k * CHUNK:(k + 1) * CHUNK]
                        last = nc.vector.tensor_tensor(m, m, bank[k][:, 0:CHUNK], ALU.add)
                    last.then_inc(gen_added, 1)
                    dve.wait_ge(gen_added, sums_before + n + 1)
                    if s == 0:
                        dve.wait_ge(gen_summed, sums_before + n + 2)
                        for k in range(8):
                            d = deg_one[0:1, k * CHUNK:(k + 1) * CHUNK]
                            last = nc.vector.tensor_tensor(d, d, bank[k][0:1, 0:CHUNK], ALU.add)
                        last.then_inc(gen_added, 1)
                        dve.wait_ge(gen_added, sums_before + n + 2)
                nc.vector.memset(marker[:, :], 0.0).then_inc(gen_group_done, 1)

            links = [0]

            def glink(ins, s, g):
                ins.then_inc(gen_link, 1)
                links[0] = links[0] % 3 + 1
                dve.wait_ge(gen_link, 3 * (s * GROUPS + g) + links[0])

            def split_first(batches):
                for b in batches:
                    t0, n = BATCHES[b]
                    dve.wait_ge(first_parts, b + 1)
                    if b >= 1:
                        dve.wait_ge(parts_ready, b)
                    split(p_parts[0][:, t0:t0 + n, :, :], stage[:, t0:t0 + n, :], b)

            flag = outside_flag(dve)
            dve.wait_ge(msg_zero, STEPS)
            for s in range(STEPS):
                with dve.If(flag == 0):
                    if s == 0:
                        split_first(range(0, 3))
                    build_picks(s, 0, 0, s == 0)
                    if s == 0:
                        dve.wait_ge(ids_ready, 2)
                        split_first(range(3, len(BATCHES)))
                        dve.wait_ge(deg_ready, 1)
                    for u in range(1 if s == 0 else U):
                        build_src_onehot(s, 0, u)
                    if s > 0:
                        split_tiles(s - 1, LOOP_TILES, TAIL_TILES)
                    windowed_iteration(s, 0, True, False)
                    with dve.Fori(1, LAG) as i:
                        windowed_iteration(s, i, False, False)
                    windowed_iteration(s, LAG, False, True, True)
                    with dve.Fori(LAG + 1, ITERS - 1) as i:
                        windowed_iteration(s, i, False, True)
                    bases = [window_base(k) for k in range(GROUPS - 3, GROUPS)]
                    windowed_iteration(s, ITERS - 1, False, True, last=True)
                    add_messages(s, bases[0], (s + 1) * GROUPS - 3, (GROUPS - 3) % U, False)
                    add_gathered(s, s * GROUPS + GROUPS - 1, rows_before(s, ITERS, U - 1), U - 1, False)
                    add_messages(s, bases[1], (s + 1) * GROUPS - 2, (GROUPS - 2) % U, False)
                    add_messages(s, bases[2], (s + 1) * GROUPS - 1, (GROUPS - 1) % U, False)
                    if s < STEPS - 1:
                        split_tiles(s, LOOP_TILES - 1)
                    update_h(s, LOOP_TILES, False, TAIL_TILES)
                with dve.Else():
                    if s == 0:
                        dve.wait_ge(all_nodes_ready, 1)
                        dve.wait_ge(deg_ready, 1)
                        nc.vector.memset(marker[:, :], 0.0).then_inc(gen_group_done, 1)
                    with dve.Fori(0, GROUPS) as g:
                        general_group(s, g)
                    dve.wait_ge(gen_group_done, (s + 1) * GROUPS + 1)
                    nc.vector.memset(marker[:, :], 0.0).then_inc(step_done, 1)
                    update_h(s, 0, s == 0)
                    with dve.Fori(1, LOOP_TILES) as t:
                        update_h(s, t, False)
                    update_h(s, LOOP_TILES, False, TAIL_TILES)


def kernel(x, src, dst, edge_attr_32, L0_gnn_We1, L0_gnn_be1, L0_gnn_We2, L0_gnn_be2, L0_gnn_bias):
    import numpy as np
    import concourse.bacc as bacc
    from concourse.bass_utils import run_bass_kernel_spmd as run

    def padded(a, rows, fill=0):
        a = np.asarray(a)
        return np.concatenate([a, np.full((rows - a.shape[0], *a.shape[1:]), fill, a.dtype)])

    src = padded(src, EP)
    dst = padded(dst, EP, N)
    row = lambda a: np.asarray(a).reshape(1, -1)
    arrays = {
        "x": padded(x, NP),
        "src_groups": np.ascontiguousarray(src.reshape(GROUPS, TILES, P).transpose(2, 0, 1)),
        "dst_groups": np.ascontiguousarray(dst.reshape(GROUPS, TILES, P).transpose(2, 0, 1)),
        "dst_row": row(dst),
        "src_row": src.reshape(ITERS, U * EDGE_GROUP),
        "group_base": row(dst[::EDGE_GROUP].copy()),
        "edge_t": np.ascontiguousarray(padded(edge_attr_32, EP).T),
        "we1": np.asarray(L0_gnn_We1), "be1": row(L0_gnn_be1), "we2": np.asarray(L0_gnn_We2),
        "be2": row(L0_gnn_be2), "bias": row(L0_gnn_bias),
    }
    nc = bacc.Bacc("TRN2", target_bir_lowering=False, num_devices=1)
    args = {k: nc.dram_tensor(k, a.shape, mybir.dt.from_np(a.dtype), kind="ExternalInput").ap()
            for k, a in arrays.items()}
    tables = {k: [nc.dram_tensor(f"{k}{s}", (NP, C), mybir.dt.float32, kind="Internal").ap() for s in range(STEPS)]
              for k in ("p_tab", "q_tab")}
    out = nc.dram_tensor("out", (NP, C), mybir.dt.float32, kind="ExternalOutput").ap()
    gnn_kernel(nc, **args, **tables, out=out)
    return run(nc, [arrays], core_ids=[0]).results[0]["out"][:N]
```
